# Optimizing a Trainium2 kernel written in Bass

```python
import numpy as np
import jax
import jax.numpy as jnp

def _softmax(x, axis=-1):
    return jax.nn.softmax(x, axis=axis)

def _gelu(x):
    return jax.nn.gelu(x, approximate=True)

def _silu(x):
    return jax.nn.silu(x)

def _sigmoid(x):
    return jax.nn.sigmoid(x)

def _layernorm(x, axis=-1, eps=1e-05):
    m = jnp.mean(x, axis=axis, keepdims=True)
    v = jnp.var(x, axis=axis, keepdims=True)
    return (x - m) / jnp.sqrt(v + eps)

def _scatter_add(tgt, idx, src, axis=0):
    return tgt.at[idx].add(src)

def _segment_sum(src, seg, n):
    return jax.ops.segment_sum(src, seg, n)
kernel_name = 'mk_sandwich_d1_jaxref_r8_04eed4'

def setup_inputs(seed: int=0):
    np.random.seed(seed)
    _w = jnp.asarray

    def _L0_attn_setup():
        import jax, jax.numpy as jnp
        import numpy as np
        D_MODEL = 128
        NUM_HEADS = 16
        D_K = D_MODEL // NUM_HEADS
        B, S = (4, 256)
        key = jax.random.key(seed)
        k1, k2, k3 = jax.random.split(key, 3)
        x = jax.random.normal(k1, (B, S, D_MODEL), dtype=jnp.float32)
        w_qkv = jax.random.normal(k2, (3, NUM_HEADS, D_K, D_MODEL), dtype=jnp.float32) / np.sqrt(D_MODEL)
        w_o = jax.random.normal(k3, (D_MODEL, D_MODEL), dtype=jnp.float32) / np.sqrt(D_MODEL)
        return {'x': x, 'w_qkv': w_qkv, 'w_o': w_o}
    _L0_attn_in = _L0_attn_setup()

    def _L0_ffn_setup():
        import jax, jax.numpy as jnp
        import numpy as np
        D_MODEL = 128
        DEPTH = 8
        M = 2 ** DEPTH
        N_INTERNAL = M - 1
        B, T = (8, 512)

        def _leaf_probs(gate):
            BT = gate.shape[0]
            lp = jnp.ones((BT, M), dtype=gate.dtype)
            for level in range(DEPTH):
                n = 2 ** level
                half = M // (2 * n)
                g = gate[:, n - 1:2 * n - 1]
                f = jnp.stack([1.0 - g, g], axis=-1)
                f = jnp.broadcast_to(f[..., None], (BT, n, 2, half))
                lp = lp * f.reshape(BT, M)
            return lp
        key = jax.random.key(seed)
        ks = jax.random.split(key, 7)
        x = jax.random.normal(ks[0], (B, T, D_MODEL), dtype=jnp.float32)
        Wq = jax.random.normal(ks[1], (D_MODEL, D_MODEL), dtype=jnp.float32) * 0.02
        routers = jax.random.normal(ks[2], (N_INTERNAL, D_MODEL), dtype=jnp.float32) * 0.02
        leaf_keys = jax.random.normal(ks[3], (M, D_MODEL), dtype=jnp.float32) * 0.02
        leaf_values = jax.random.normal(ks[4], (M, D_MODEL), dtype=jnp.float32) * 0.02
        Wout_w = jax.random.normal(ks[5], (D_MODEL, D_MODEL), dtype=jnp.float32) * 0.02
        Wout_b = jax.random.normal(ks[6], (D_MODEL,), dtype=jnp.float32) * 0.02
        return {'x': x, 'Wq': Wq, 'routers': routers, 'leaf_keys': leaf_keys, 'leaf_values': leaf_values, 'Wout_w': Wout_w, 'Wout_b': Wout_b}
    _L0_ffn_in = _L0_ffn_setup()
    _d = {'L0_attn_x': _L0_attn_in['x'], 'L0_attn_w_qkv': _L0_attn_in['w_qkv'], 'L0_attn_w_o': _L0_attn_in['w_o'], 'L0_ffn_Wq': _L0_ffn_in['Wq'], 'L0_ffn_routers': _L0_ffn_in['routers'], 'L0_ffn_leaf_keys': _L0_ffn_in['leaf_keys'], 'L0_ffn_leaf_values': _L0_ffn_in['leaf_values'], 'L0_ffn_Wout_w': _L0_ffn_in['Wout_w'], 'L0_ffn_Wout_b': _L0_ffn_in['Wout_b']}
    _x0 = _d['L0_attn_x']
    _d['L0_attn_x'] = jax.random.normal(jax.random.fold_in(jax.random.key(seed), 1), (32, 256, 128), dtype=_x0.dtype)
    del _x0
    return _d

def reference(L0_attn_x, L0_attn_w_qkv, L0_attn_w_o, L0_ffn_Wq, L0_ffn_routers, L0_ffn_leaf_keys, L0_ffn_leaf_values, L0_ffn_Wout_w, L0_ffn_Wout_b):

    def _L0_attn_ref(x, w_qkv, w_o):
        import jax, jax.numpy as jnp
        import numpy as np
        D_MODEL = 128
        NUM_HEADS = 16
        D_K = D_MODEL // NUM_HEADS
        B, S = (4, 256)
        seq_len = x.shape[-2]
        d_k = w_qkv.shape[-2]
        qkv = jnp.einsum('bsm,qhkm->qbhsk', x, w_qkv)
        Q, K, V = (qkv[0], qkv[1], qkv[2])
        scores = jnp.einsum('bhsk,bhtk->bhst', Q, K) / jnp.sqrt(jnp.asarray(d_k, x.dtype))
        causal = jnp.tril(jnp.ones((seq_len, seq_len), dtype=bool))
        scores = jnp.where(causal, scores, -jnp.inf)
        probs = jax.nn.softmax(scores, axis=-1)
        attn = jnp.einsum('bhst,bhtk->bhsk', probs, V)
        b, h, s, k = attn.shape
        attn_cat = jnp.transpose(attn, (0, 2, 1, 3)).reshape(b, s, h * k)
        return jnp.einsum('bsd,md->bsm', attn_cat, w_o)

    def _L0_ffn_ref(x, Wq, routers, leaf_keys, leaf_values, Wout_w, Wout_b):
        import jax, jax.numpy as jnp
        import numpy as np
        D_MODEL = 128
        DEPTH = 8
        M = 2 ** DEPTH
        N_INTERNAL = M - 1
        B, T = (8, 512)

        def _leaf_probs(gate):
            BT = gate.shape[0]
            lp = jnp.ones((BT, M), dtype=gate.dtype)
            for level in range(DEPTH):
                n = 2 ** level
                half = M // (2 * n)
                g = gate[:, n - 1:2 * n - 1]
                f = jnp.stack([1.0 - g, g], axis=-1)
                f = jnp.broadcast_to(f[..., None], (BT, n, 2, half))
                lp = lp * f.reshape(BT, M)
            return lp
        Bv, Tv, d = x.shape
        q = jnp.einsum('btd,ed->bte', x, Wq)
        q_flat = q.reshape(Bv * Tv, d)
        gate = jax.nn.sigmoid(q_flat @ routers.T)
        leaf_prob = _leaf_probs(gate)
        ret = (leaf_prob @ leaf_values).reshape(Bv, Tv, d)
        return jnp.einsum('btd,ed->bte', ret, Wout_w) + Wout_b
    x = L0_attn_x
    x = x + _layernorm(_L0_attn_ref(_layernorm(x, axis=-1), L0_attn_w_qkv, L0_attn_w_o), axis=-1)
    x = x + _layernorm(_L0_ffn_ref(_layernorm(x, axis=-1), L0_ffn_Wq, L0_ffn_routers, L0_ffn_leaf_keys, L0_ffn_leaf_values, L0_ffn_Wout_w, L0_ffn_Wout_b), axis=-1)
    return x

_drawn_inputs = setup_inputs


def setup_inputs(seed=0):
    import zlib

    import numpy as np

    out = dict(_drawn_inputs(seed))
    spreads = {}
    factors = {'L0_ffn_Wq': 8.0,
     'L0_ffn_routers': 8.0,
     'L0_ffn_leaf_values': 7.314,
     'L0_ffn_Wout_w': 7.051}
    for name, (base, spread) in spreads.items():
        noise = np.random.default_rng([zlib.crc32(name.encode()), seed]).standard_normal(out[name].shape)
        drawn = base * np.exp(spread * noise) if base else spread * noise
        out[name] = jnp.asarray(drawn.astype(out[name].dtype))
    for name, factor in factors.items():
        out[name] = (out[name] * factor).astype(out[name].dtype)
    return out
```

```python
from contextlib import ExitStack

import numpy as np

import concourse.bass as bass
from concourse import mybir

ALU = mybir.AluOpType
ACT = mybir.ActivationFunctionType
AX_X = mybir.AxisListType.X
F32 = mybir.dt.float32
BF16 = mybir.dt.bfloat16

BATCHES, SEQ, D = 32, 256, 128
HEADS, DK = 16, 8
TILE = 128
PAIRS = HEADS // 2
LEVELS = 8
NODES = 2**LEVELS - 1
GATES = NODES + 1
HALF = 2 ** (LEVELS - 1)
EPS = 1e-5
MASKED = -3.0e38
PARTS = ((0, 0), (1, 0), (2, 0), (0, 1), (1, 1), (0, 2))
STACK = len(PARTS) * 2 * DK
MROWS = 3
BANK = 512
UNITS = 12
SLOTS = 12
TURN = 4

T_LOAD = 0
T_LN1_STATS, T_LN1_NORM = 6, 8
J_XT = 12
J_QK, T_QK_REST, T_QK_LOW, T_STACK = 14, 15, 16, 18
J_V = 15
T_MAX = 27
J_M, T_MROWS = 40, 41
T_EXP = 46
T_CAUSAL0, T_CAUSAL1 = 47, 48
T_PV = 51
T_RELOAD = 60
J_O = (58, 65)
J_OT, J_Y = 67, 69
T_LN2_STATS, T_LN2_NORM, T_X1 = 70, 72, 73
T_LN3_STATS, T_LN3_NORM = 74, 76
J_X1T, J_Z = 78, 80
T_TREE = 81
J_LPT, J_RET = 85, 95
T_LN4_STATS, T_LN4_NORM, T_OUT, T_STORE = 96, 98, 99, 100
MISC_JOBS = (J_XT, J_QK, J_V, J_M, J_O[0], J_O[1], J_OT, J_Y, J_X1T, J_Z, J_LPT, J_RET)
LAST = T_STORE // SLOTS
ITERATIONS = BATCHES + LAST
LOOP_FROM, LOOP_TO = 8, 32
assert LOOP_FROM >= LAST and LOOP_TO <= BATCHES and LOOP_FROM % TURN == 0 and LOOP_TO % TURN == 0
assert sorted(t % SLOTS for t in MISC_JOBS) == list(range(SLOTS))


class Batch:

    def __init__(self, turn, at):
        self.turn, self.at = turn, at
        self.least = (turn if isinstance(turn, int) else LOOP_FROM // TURN) * TURN + at
        self.index = turn * TURN + at
        self.live = 0 <= self.least < BATCHES
        self.two, self.four = at % 2, at % 4

    def has(self, back):
        return self.least >= back

    def count(self, per, plus):
        return self.turn * (TURN * per) + (self.at * per + plus)

    def turns_of(self, ring, per, back=0):
        return self.turn * (TURN // ring * per) + ((self.at - back) // ring + 1) * per


class Step:

    def __init__(self, turn, at):
        self.turn, self.at = turn, at
        self.least = (turn if isinstance(turn, int) else LOOP_FROM // TURN) * TURN + at

    def batch(self, slot, time):
        if (time - slot) % SLOTS:
            return None
        b = Batch(self.turn, self.at - (time - slot) // SLOTS)
        return b if b.live else None


def steps(eng):
    for i in range(LOOP_FROM):
        yield Step(i // TURN, i % TURN)
    with eng.Fori(LOOP_FROM // TURN, LOOP_TO // TURN) as turn:
        for u in range(TURN):
            yield Step(turn, u)
    for i in range(LOOP_TO, ITERATIONS):
        yield Step(i // TURN, i % TURN)


def sandwich_kernel(nc, x, w_qkv, w_o, Wq, routers, leaf_keys, leaf_values, Wout_w, Wout_b, out):
    x_v = x.rearrange("b (t p) d -> b p t d", p=TILE)
    out_v = out.rearrange("b (t p) d -> b p t d", p=TILE)

    with ExitStack() as ctx:
        def sb(name, shape, dt=F32):
            return ctx.enter_context(nc.sbuf_tensor(name, shape, dt))

        def sem(name):
            return ctx.enter_context(nc.semaphore(name))

        misc = [ctx.enter_context(nc.psum_tensor(f"misc{i}", [128, BANK], F32)) for i in range(2)]
        smax = [ctx.enter_context(nc.psum_tensor(f"smax{i}", [128, BANK], F32)) for i in range(2)]
        sexp = [ctx.enter_context(nc.psum_tensor(f"sexp{i}", [128, BANK], F32)) for i in range(2)]
        pvps = [ctx.enter_context(nc.psum_tensor(f"pvps{i}", [128, BANK], F32)) for i in range(2)]

        ident = sb("ident", [128, 128])
        identb = sb("identb", [128, 128], BF16)
        mask = sb("mask", [128, 128], BF16)
        onesb = sb("onesb", [128, 128], BF16)
        neghalf = sb("neghalf", [128, 2])
        eps = sb("eps", [128, 2])
        zero2 = sb("zero2", [128, 2])
        wraw = sb("wraw", [128, 9, 128])
        wT = sb("wT", [128, 9, 128])
        rraw = sb("rraw", [127, 128])
        rT = sb("rT", [128, GATES])
        wqk = sb("wqk", [128, 2, 128])
        wg = sb("wg", [128, GATES])
        lva = sb("lva", [128, 128])
        lvb = sb("lvb", [128, 128])
        lvd = sb("lvd", [128, 128])
        bias0 = sb("bias0", [1, 128])
        bias_r = sb("bias_r", [1, 2, 128])
        bias_p = sb("bias_p", [1, 3, 128], BF16)
        biasb = sb("biasb", [128, 128], BF16)

        xin = [sb(f"xin{i}", [128, 2, 128]) for i in range(2)]
        xn = [sb(f"xn{i}", [128, 2, 128]) for i in range(2)]
        xT = [sb(f"xT{i}", [128, 256]) for i in range(2)]
        parts = [sb(f"parts{i}", [128, 6, 256], BF16) for i in range(2)]
        rest = [sb(f"rest{i}", [128, 2, 256]) for i in range(2)]
        qsec = [sb(f"qsec{i}", [128, 3, 2, 256], BF16) for i in range(2)]
        qs = [sb(f"qs{i}", [128, PAIRS, 2, 256], BF16) for i in range(4)]
        kd = [sb(f"kd{i}", [128, PAIRS, 256], BF16) for i in range(4)]
        vaug = [sb(f"vaug{i}", [128, 2, HEADS, 32]) for i in range(4)]
        mx = [sb(f"mx{i}", [128, HEADS, 2]) for i in range(2)]
        mrest = [sb(f"mrest{i}", [32, 128]) for i in range(2)]
        mparts = [sb(f"mparts{i}", [32, 3, 128], BF16) for i in range(2)]
        probs = [sb(f"probs{i}", [128, UNITS, BANK]) for i in range(2)]
        oraw = [sb(f"oraw{i}", [128, 2, BANK]) for i in range(2)]
        rden = [sb(f"rden{i}", [128, 2, HEADS]) for i in range(2)]
        onorm = [sb(f"onorm{i}", [128, 2, HEADS, DK]) for i in range(2)]
        oT = [sb(f"oT{i}", [128, 256]) for i in range(2)]
        y = [sb(f"y{i}", [128, 2, 128]) for i in range(2)]
        yn = [sb(f"yn{i}", [128, 2, 128]) for i in range(2)]
        xres = [sb(f"xres{i}", [128, 2, 128]) for i in range(2)]
        x1 = [sb(f"x1{i}", [128, 2, 128]) for i in range(4)]
        x1n = [sb(f"x1n{i}", [128, 2, 128]) for i in range(2)]
        x1T = [sb(f"x1T{i}", [128, 256]) for i in range(2)]
        u = [sb(f"u{i}", [128, 2, GATES]) for i in range(2)]
        tree = [sb(f"tree{i}", [128, 2, 256]) for i in range(2)]
        right = [sb(f"right{i}", [128, 2, HALF]) for i in range(2)]
        lpT = [sb(f"lpT{i}", [128, 2, 2, 128]) for i in range(2)]
        ret = [sb(f"ret{i}", [128, 2, 128]) for i in range(2)]
        retn = [sb(f"retn{i}", [128, 2, 128]) for i in range(2)]
        outb = [sb(f"outb{i}", [128, 2, 128]) for i in range(2)]
        stats = [[sb(f"stats{k}_{i}", [128, 2, 6]) for i in range(2)] for k in range(4)]
        mv = [[sb(f"mv{k}_{i}", [128, 2, 2]) for i in range(2)] for k in range(4)]
        vare = [[sb(f"vare{k}_{i}", [128, 2]) for i in range(2)] for k in range(4)]
        rstd = [[sb(f"rstd{k}_{i}", [128, 2]) for i in range(2)] for k in range(4)]
        mr = [[sb(f"mr{k}_{i}", [128, 2]) for i in range(2)] for k in range(4)]
        nmr = [[sb(f"nmr{k}_{i}", [128, 2]) for i in range(2)] for k in range(4)]

        w_loaded = sem("w_loaded")
        bias_loaded = sem("bias_loaded")
        bias_placed = sem("bias_placed")
        zeroed = sem("zeroed")
        const_ready = sem("const_ready")
        vset = sem("vset")
        w_turned = sem("w_turned")
        w_copied = sem("w_copied")
        w_fused = sem("w_fused")
        lv_step = sem("lv_step")
        w_ready = sem("w_ready")
        bias_step = sem("bias_step")
        buffers_set = sem("buffers_set")

        x_loaded = [sem(f"x_loaded{i}") for i in range(2)]
        xres_loaded = [sem(f"xres_loaded{i}") for i in range(2)]
        stacked = [sem(f"stacked{i}") for i in range(4)]
        mrows_in = [sem(f"mrows_in{i}") for i in range(2)]
        stored = [sem(f"stored{i}") for i in range(2)]
        stats_done = [sem(f"stats_done{k}") for k in range(4)]
        mv_ready = [sem(f"mv_ready{k}") for k in range(4)]
        rstd_step = [sem(f"rstd_step{k}") for k in range(4)]
        xn_ready = sem("xn_ready")
        xT_ps = sem("xT_ps")
        xT_ready = sem("xT_ready")
        qk_ps = sem("qk_ps")
        v_ps = sem("v_ps")
        hi_ready = sem("hi_ready")
        rest_ready = sem("rest_ready")
        mid_ready = sem("mid_ready")
        lo_ready = sem("lo_ready")
        qsec_ready = sem("qsec_ready")
        v_ready = sem("v_ready")
        smax_ps = sem("smax_ps")
        max_done = sem("max_done")
        m_ps = sem("m_ps")
        m_step = sem("m_step")
        sexp_ps = sem("sexp_ps")
        exp_done = sem("exp_done")
        causal_done = sem("causal_done")
        pv_ps = sem("pv_ps")
        oraw_ready = sem("oraw_ready")
        o_ps = sem("o_ps")
        rden_ready = sem("rden_ready")
        onorm_ready = sem("onorm_ready")
        oT_ps = sem("oT_ps")
        oT_ready = sem("oT_ready")
        y_ps = sem("y_ps")
        y_ready = sem("y_ready")
        yn_ready = sem("yn_ready")
        x1_ready = sem("x1_ready")
        x1n_ready = sem("x1n_ready")
        x1T_ps = sem("x1T_ps")
        x1T_ready = sem("x1T_ready")
        z_ps = sem("z_ps")
        u_ready = sem("u_ready")
        tree_step = sem("tree_step")
        lpT_ps = sem("lpT_ps")
        lpT_ready = sem("lpT_ready")
        ret_ps = sem("ret_ps")
        ret_ready = sem("ret_ready")
        retn_ready = sem("retn_ready")
        out_ready = sem("out_ready")
        TREE = 2 * (LEVELS - 1) + 1

        w_src = [w_qkv[i].rearrange("h k m -> (h k) m") for i in range(3)] + [
            w_o, Wout_w, Wq, routers[0:128, :], leaf_values[0:128, :], leaf_values[128:256, :]]
        W_Q, W_K, W_V, W_O, W_OUT, W_FQ, W_R0, W_L0, W_L1 = range(9)

        block = ctx.enter_context(nc.Block())

        @block.sync
        def _(sp):
            for j, src in enumerate(w_src):
                sp.dma_start(wraw[:, j, :], src).then_inc(w_loaded, 16)
            sp.dma_start(rraw[:, :], routers[128:NODES, :]).then_inc(w_loaded, 16)
            sp.dma_start(bias0[:, :], Wout_b.rearrange("(a d) -> a d", a=1)).then_inc(bias_loaded, 16)
            sp.wait_ge(bias_step, 5)
            sp.dma_start(biasb[0:3, :], bias_p[:, :, :]).then_inc(bias_placed, 16)

            for st in steps(sp):
                for slot in range(SLOTS):
                    b = st.batch(slot, T_LOAD)
                    if b:
                        if b.has(2):
                            sp.wait_ge(xn_ready, b.count(2, -2))
                        sp.dma_start(xin[b.two][:, :, :], x_v[b.index]).then_inc(x_loaded[b.two], 16)
                    b = st.batch(slot, T_STACK)
                    if b:
                        if b.has(4):
                            sp.wait_ge(sexp_ps, b.count(UNITS, -3 * UNITS))
                        for j, (_, part) in enumerate(PARTS):
                            if part == 0:
                                sp.wait_ge(hi_ready, b.count(1, 1))
                            elif part == 1:
                                sp.wait_ge(mid_ready, b.count(1, 1))
                            else:
                                sp.wait_ge(lo_ready, b.count(1, 1))
                            sp.dma_start(kd[b.four][16 * j:16 * j + 16, :, :],
                                         parts[b.two][:, 5 - part, :]).then_inc(stacked[b.four], 16)
                        sp.wait_ge(qsec_ready, b.count(2, 2))
                        for j, (part, _) in enumerate(PARTS):
                            sp.dma_start(qs[b.four][16 * j:16 * j + 16, :, :, :].rearrange("p h s t -> p h (s t)"),
                                         qsec[b.two][:, part, :, :].rearrange("p s t -> p (s t)")
                                         ).then_inc(stacked[b.four], 16)
                    b = st.batch(slot, T_MROWS)
                    if b:
                        sp.wait_ge(m_step, b.count(4, 4))
                        for j in range(MROWS):
                            sp.dma_start(qs[b.four][STACK + j:STACK + j + 1, :, :, :].rearrange("p h s t -> p (h s t)"),
                                         mparts[b.two][:, j, :]).then_inc(mrows_in[b.two], 16)
                    b = st.batch(slot, T_RELOAD)
                    if b:
                        if b.has(2):
                            sp.wait_ge(x1_ready, b.count(1, -1))
                        sp.dma_start(xres[b.two][:, :, :], x_v[b.index]).then_inc(xres_loaded[b.two], 16)
                    b = st.batch(slot, T_STORE)
                    if b:
                        sp.wait_ge(out_ready, b.count(1, 1))
                        sp.dma_start(out_v[b.index], outb[b.two][:, :, :]).then_inc(stored[b.two], 16)
            for i in range(2):
                sp.wait_ge(stored[i], 16 * (BATCHES // 2))

        @block.gpsimd
        def _(pool):
            nc.gpsimd.memset(ident[:, :], 0.0).then_inc(zeroed, 1)
            nc.gpsimd.memset(identb[:, :], 0.0).then_inc(zeroed, 1)
            nc.gpsimd.memset(mask[:, :], 0.0).then_inc(zeroed, 1)
            nc.gpsimd.memset(onesb[:, :], 0.0).then_inc(zeroed, 1)
            nc.gpsimd.memset(neghalf[:, :], -0.5).then_inc(const_ready, 1)
            nc.gpsimd.memset(eps[:, :], EPS).then_inc(zeroed, 1)
            nc.gpsimd.memset(zero2[:, :], 0.0).then_inc(const_ready, 1)
            pool.wait_ge(zeroed, 5)
            nc.gpsimd.affine_select(out=ident[:, :], in_=ident[:, :], compare_op=ALU.not_equal, fill=1.0,
                                    base=0, pattern=[[-1, 128]], channel_multiplier=1).then_inc(const_ready, 1)
            nc.gpsimd.affine_select(out=identb[:, :], in_=identb[:, :], compare_op=ALU.not_equal, fill=1.0,
                                    base=0, pattern=[[-1, 128]], channel_multiplier=1).then_inc(const_ready, 1)
            nc.gpsimd.affine_select(out=mask[:, :], in_=mask[:, :], compare_op=ALU.is_ge, fill=MASKED,
                                    base=0, pattern=[[-1, 128]], channel_multiplier=1).then_inc(const_ready, 1)
            nc.gpsimd.affine_select(out=onesb[:, :], in_=onesb[:, :], compare_op=ALU.is_ge, fill=1.0,
                                    base=-3, pattern=[[0, 128]], channel_multiplier=1).then_inc(const_ready, 1)

            def rstd_of(k, b, steps_each):
                pool.wait_ge(mv_ready[k], b.count(2, 2))
                two, step = b.two, rstd_step[k]
                nc.gpsimd.tensor_tensor(vare[k][two][:, :], mv[k][two][:, :, 1], eps[:, :],
                                        ALU.add).then_inc(step, 1)
                pool.wait_ge(step, b.count(steps_each, 1))
                nc.gpsimd.tensor_tensor(rstd[k][two][:, :], vare[k][two][:, :], neghalf[:, :],
                                        ALU.pow).then_inc(step, 1)
                if steps_each == 4:
                    pool.wait_ge(step, b.count(4, 2))
                    nc.gpsimd.tensor_tensor(mr[k][two][:, :], mv[k][two][:, :, 0], rstd[k][two][:, :],
                                            ALU.mult).then_inc(step, 1)
                    pool.wait_ge(step, b.count(4, 3))
                    nc.gpsimd.tensor_tensor(nmr[k][two][:, :], zero2[:, :], mr[k][two][:, :],
                                            ALU.subtract).then_inc(step, 1)

            def causal(b, units, view):
                pool.wait_ge(exp_done, b.count(UNITS, units))
                pool.nop(nofuse=True)
                nc.gpsimd.affine_select(out=view, in_=view, compare_op=ALU.is_ge, fill=0.0, base=0,
                                        pattern=[[0, 4], [1, 128]], channel_multiplier=-1
                                        ).then_inc(causal_done, 1)

            for st in steps(pool):
                for slot in range(SLOTS):
                    b = st.batch(slot, T_LN1_STATS)
                    if b:
                        rstd_of(0, b, 2)
                    b = st.batch(slot, T_QK_LOW)
                    if b:
                        pool.wait_ge(mid_ready, b.count(1, 1))
                        nc.gpsimd.tensor_tensor(parts[b.two][:, 2:4, :], rest[b.two][:, :, :],
                                                parts[b.two][:, 1:5:3, :], ALU.subtract).then_inc(lo_ready, 1)
                    for g in range(4):
                        b = st.batch(slot, T_CAUSAL0 + 3 * g)
                        if b:
                            causal(b, 3 * g + 2, probs[b.two][:, 3 * g:3 * g + 2, :].rearrange(
                                "p u (h s) -> p (u h) s", h=2)[:, :, 0:128])
                        b = st.batch(slot, T_CAUSAL1 + 3 * g)
                        if b:
                            causal(b, 3 * g + 3, probs[b.two][:, 3 * g + 2, :].rearrange(
                                "p (h s) -> p h s", h=4))
                    b = st.batch(slot, T_LN2_STATS)
                    if b:
                        rstd_of(1, b, 4)
                    b = st.batch(slot, T_X1)
                    if b:
                        pool.wait_ge(yn_ready, b.count(2, 2))
                        pool.wait_ge(xres_loaded[b.two], b.turns_of(2, 16))
                        nc.gpsimd.tensor_tensor(x1[b.four][:, :, :], xres[b.two][:, :, :], yn[b.two][:, :, :],
                                                ALU.add).then_inc(x1_ready, 1)
                    b = st.batch(slot, T_LN3_STATS)
                    if b:
                        rstd_of(2, b, 2)
                    b = st.batch(slot, T_LN4_STATS)
                    if b:
                        rstd_of(3, b, 4)
                    b = st.batch(slot, T_OUT)
                    if b:
                        pool.wait_ge(retn_ready, b.count(2, 2))
                        if b.has(2):
                            pool.wait_ge(stored[b.two], b.turns_of(2, 16, 2))
                        nc.gpsimd.tensor_tensor(outb[b.two][:, :, :], x1[b.four][:, :, :], retn[b.two][:, :, :],
                                                ALU.add).then_inc(out_ready, 1)

        @block.scalar
        def _(act):
            def copy(dst, src):
                return nc.scalar.activation(dst, src, ACT.Copy)

            act.wait_ge(w_turned, 1)
            copy(wT[:, W_V, :], misc[0][:, 256:384]).then_inc(w_copied, 1)
            for j in (W_Q, W_K):
                copy(wqk[:, j, :].rearrange("p (a d h) -> p a d h", a=2, d=DK),
                     misc[0][:, 128 * j:128 * j + 128].rearrange("p (h a d) -> p a d h", a=2, d=DK)
                     ).then_inc(w_copied, 1)
            copy(wT[:, W_O, :], misc[0][:, 384:512]).then_inc(w_copied, 1)
            act.wait_ge(w_turned, 2)
            copy(rT[:, 0:128], misc[1][:, 0:128]).then_inc(w_copied, 1)
            copy(wT[:, W_L0:W_L1 + 1, :].rearrange("p a n -> p (a n)"), misc[1][:, 128:384]).then_inc(w_copied, 1)
            copy(wT[:, W_OUT, :], misc[1][:, 384:512]).then_inc(w_copied, 1)
            act.wait_ge(w_turned, 3)
            copy(rT[:, 128:NODES], smax[0][:, 0:127]).then_inc(w_copied, 1)
            act.wait_ge(w_fused, 1)
            copy(wg[:, 0:NODES], smax[1][:, 0:NODES]).then_inc(w_ready, 1)

            def normalise(k, b, dst, src):
                for t in range(2):
                    nc.scalar.activation(dst[b.two][:, t, :], src[b.two][:, t, :], ACT.Identity,
                                         bias=nmr[k][b.two][:, t:t + 1], scale=rstd[k][b.two][:, t:t + 1]
                                         ).then_inc(yn_ready if k == 1 else retn_ready, 1)

            for st in steps(act):
                for slot in range(SLOTS):
                    b = st.batch(slot, J_XT)
                    if b:
                        act.wait_ge(xT_ps, b.count(1, 1))
                        if b.has(2):
                            act.wait_ge(v_ps, b.count(1, -1))
                        copy(xT[b.two][:, :], misc[slot % 2][:, 0:256]).then_inc(xT_ready, 1)
                    b = st.batch(slot, J_QK)
                    if b:
                        act.wait_ge(qk_ps, b.count(1, 1))
                        if b.has(2):
                            act.wait_ge(stacked[(b.four + 2) % 4], b.turns_of(4, 16 * 12, 2))
                        copy(parts[b.two][:, 0::5, :], misc[slot % 2][:, :].rearrange("p (a n) -> p a n", a=2)
                             ).then_inc(hi_ready, 1)
                    b = st.batch(slot, T_QK_LOW)
                    if b:
                        act.wait_ge(rest_ready, b.count(1, 1))
                        copy(parts[b.two][:, 1:5:3, :], rest[b.two][:, :, :]).then_inc(mid_ready, 1)
                    b = st.batch(slot, J_V)
                    if b:
                        act.wait_ge(v_ps, b.count(1, 1))
                        if b.has(4):
                            act.wait_ge(pv_ps, b.count(4, -12))
                        else:
                            act.wait_ge(buffers_set, 1)
                        copy(vaug[b.four][:, :, :, 0:DK],
                             misc[slot % 2][:, 0:256].rearrange("p (t h d) -> p t h d", t=2, d=DK)
                             ).then_inc(v_ready, 1)
                    for g in (1, 3):
                        b = st.batch(slot, T_PV + 3 * g)
                        if b:
                            act.wait_ge(pv_ps, b.count(4, g + 1))
                            if b.has(2):
                                act.wait_ge(o_ps, b.count(2, -4 + g // 2 + 1))
                            copy(oraw[b.two][:, g // 2, :], pvps[g // 2][:, :]).then_inc(oraw_ready, 1)
                    b = st.batch(slot, J_OT)
                    if b:
                        act.wait_ge(oT_ps, b.count(1, 1))
                        if b.has(2):
                            act.wait_ge(y_ps, b.count(1, -1))
                        copy(oT[b.two][:, :], misc[slot % 2][:, 0:256]).then_inc(oT_ready, 1)
                    b = st.batch(slot, J_Y)
                    if b:
                        act.wait_ge(y_ps, b.count(1, 1))
                        copy(y[b.two][:, :, :].rearrange("p t n -> p (t n)"), misc[slot % 2][:, 0:256]
                             ).then_inc(y_ready, 1)
                    b = st.batch(slot, T_LN2_NORM)
                    if b:
                        act.wait_ge(rstd_step[1], b.count(4, 4))
                        if b.has(2):
                            act.wait_ge(x1_ready, b.count(1, -1))
                        normalise(1, b, yn, y)
                    b = st.batch(slot, J_X1T)
                    if b:
                        act.wait_ge(x1T_ps, b.count(1, 1))
                        if b.has(2):
                            act.wait_ge(z_ps, b.count(1, -1))
                        copy(x1T[b.two][:, :], misc[slot % 2][:, 0:256]).then_inc(x1T_ready, 1)
                    b = st.batch(slot, J_Z)
                    if b:
                        act.wait_ge(z_ps, b.count(1, 1))
                        if b.has(2):
                            act.wait_ge(tree_step, b.count(TREE, -TREE))
                        nc.scalar.activation(u[b.two][:, :, :].rearrange("p t n -> p (t n)"), misc[slot % 2][:, :],
                                             ACT.Tanh, scale=0.5).then_inc(u_ready, 1)
                    b = st.batch(slot, J_LPT)
                    if b:
                        act.wait_ge(lpT_ps, b.count(1, 1))
                        if b.has(2):
                            act.wait_ge(ret_ps, b.count(1, -1))
                        copy(lpT[b.two][:, :, :, :].rearrange("p t a n -> p (t a n)"), misc[slot % 2][:, :]
                             ).then_inc(lpT_ready, 1)
                    b = st.batch(slot, J_RET)
                    if b:
                        act.wait_ge(ret_ps, b.count(1, 1))
                        copy(ret[b.two][:, :, :].rearrange("p t n -> p (t n)"), misc[slot % 2][:, 0:256]
                             ).then_inc(ret_ready, 1)
                    b = st.batch(slot, T_LN4_NORM)
                    if b:
                        act.wait_ge(rstd_step[3], b.count(4, 4))
                        if b.has(2):
                            act.wait_ge(out_ready, b.count(1, -1))
                        normalise(3, b, retn, ret)
                    for n in range(UNITS):
                        b = st.batch(slot, T_EXP + n)
                        if b:
                            act.wait_ge(sexp_ps, b.count(UNITS, n + 1))
                            if b.has(2):
                                act.wait_ge(pv_ps, b.count(4, -8 + n // 3 + 1))
                            nc.scalar.activation(probs[b.two][:, n, :], sexp[n % 2][:, :], ACT.Exp,
                                                 scale=float(DK) ** -0.5).then_inc(exp_done, 1)

        @block.vector
        def _(dve):
            for i in range(4):
                nc.vector.memset(vaug[i][:, :, :, :], 0.0).then_inc(vset, 1)
                nc.vector.memset(kd[i][96:128, :, :], -1.0).then_inc(vset, 1)
            for i in range(2):
                nc.vector.memset(qsec[i][:, :, :, :], 0.0).then_inc(vset, 1)
            nc.vector.memset(biasb[:, :], 0.0).then_inc(vset, 1)
            nc.vector.memset(wg[:, NODES:GATES], 0.0).then_inc(vset, 1)
            dve.wait_ge(vset, 12)
            for i in range(4):
                last = nc.vector.memset(vaug[i][:, :, :, DK:DK + 1], 1.0)
            last.then_inc(buffers_set, 1)
            dve.wait_ge(bias_loaded, 16)
            for j in range(3):
                src = bias0[:, :] if j == 0 else bias_r[:, j - 1, :]
                nc.vector.tensor_copy(bias_p[:, j, :], src).then_inc(bias_step, 1)
                if j < 2:
                    dve.wait_ge(bias_step, 2 * j + 1)
                    nc.vector.tensor_tensor(bias_r[:, j, :], src, bias_p[:, j, :], ALU.subtract).then_inc(bias_step, 1)
                    dve.wait_ge(bias_step, 2 * j + 2)
            dve.wait_ge(w_fused, 2)
            nc.vector.tensor_scalar(lva[:, :], sexp[0][:, 0:128], 0.5 ** (LEVELS - 1), None, ALU.mult).then_inc(lv_step, 1)
            nc.vector.tensor_scalar(lvd[:, :], sexp[0][:, 128:256], 0.5 ** LEVELS, None, ALU.mult).then_inc(lv_step, 1)
            dve.wait_ge(lv_step, 2)
            nc.vector.scalar_tensor_tensor(out=lvb[:, :], in0=lva[:, :], scalar=-0.5, in1=lvd[:, :],
                                           op0=ALU.mult, op1=ALU.add).then_inc(w_ready, 1)

            def stats_of(k, b, src):
                two = b.two
                for t in range(2):
                    nc.vector.bn_stats(stats[k][two][:, t, :], src[:, t, :]).then_inc(stats_done[k], 1)
                for t in range(2):
                    dve.wait_ge(stats_done[k], b.count(2, t + 1))
                    dve.nop(nofuse=True)
                    nc.vector.bn_aggr(mv[k][two][:, t, :], stats[k][two][:, t, :]).then_inc(mv_ready[k], 1)

            def normalise(k, b, dst, src, ready):
                for t in range(2):
                    nc.vector.tensor_scalar(dst[:, t, :], src[:, t, :], mv[k][b.two][:, t, 0:1],
                                            rstd[k][b.two][:, t:t + 1], ALU.subtract, ALU.mult).then_inc(ready, 1)

            for st in steps(dve):
                for slot in range(SLOTS):
                    b = st.batch(slot, T_LN1_STATS)
                    if b:
                        dve.wait_ge(x_loaded[b.two], b.turns_of(2, 16))
                        stats_of(0, b, xin[b.two])
                    b = st.batch(slot, T_LN1_NORM)
                    if b:
                        dve.wait_ge(rstd_step[0], b.count(2, 2))
                        if b.has(2):
                            dve.wait_ge(xT_ps, b.count(1, -1))
                        normalise(0, b, xn[b.two], xin[b.two], xn_ready)
                    b = st.batch(slot, T_QK_REST)
                    if b:
                        dve.wait_ge(hi_ready, b.count(1, 1))
                        if b.has(2):
                            dve.wait_ge(lo_ready, b.count(1, -1))
                        nc.vector.tensor_tensor(rest[b.two][:, :, :],
                                                misc[J_QK % 2][:, :].rearrange("p (a n) -> p a n", a=2),
                                                parts[b.two][:, 0::5, :], ALU.subtract).then_inc(rest_ready, 1)
                    b = st.batch(slot, T_STACK)
                    if b:
                        dve.wait_ge(lo_ready, b.count(1, 1))
                        for ab in range(2):
                            rows = slice(64 * ab, 64 * ab + 64)
                            nc.vector.tensor_copy(qsec[b.two][rows, :, ab, :], parts[b.two][rows, 0:3, :]
                                                  ).then_inc(qsec_ready, 1)
                    b = st.batch(slot, J_M)
                    if b:
                        two, src = b.two, misc[slot % 2][0:32, 0:128]
                        dve.wait_ge(m_ps, b.count(1, 1))
                        if b.has(2):
                            dve.wait_ge(mrows_in[two], b.turns_of(2, 48, 2))
                        nc.vector.tensor_copy(mparts[two][:, 0, :], src).then_inc(m_step, 1)
                        dve.wait_ge(m_step, b.count(4, 1))
                        nc.vector.tensor_tensor(mrest[two][:, :], src, mparts[two][:, 0, :], ALU.subtract
                                                ).then_inc(m_step, 1)
                        dve.wait_ge(m_step, b.count(4, 2))
                        nc.vector.tensor_copy(mparts[two][:, 1, :], mrest[two][:, :]).then_inc(m_step, 1)
                        dve.wait_ge(m_step, b.count(4, 3))
                        nc.vector.tensor_tensor(mparts[two][:, 2, :], mrest[two][:, :], mparts[two][:, 1, :],
                                                ALU.subtract).then_inc(m_step, 1)
                    for x in range(2):
                        b = st.batch(slot, J_O[x])
                        if b:
                            o = misc[slot % 2][:, :].rearrange("p (t h c) -> p t h c", t=2, h=8)
                            den = rden[b.two][:, :, 8 * x:8 * x + 8]
                            dve.wait_ge(o_ps, b.count(2, x + 1))
                            nc.vector.reciprocal(den, o[:, :, :, DK]).then_inc(rden_ready, 1)
                            dve.wait_ge(rden_ready, b.count(2, x + 1))
                            if b.has(2):
                                dve.wait_ge(oT_ps, b.count(1, -1))
                            nc.vector.tensor_tensor(onorm[b.two][:, :, 8 * x:8 * x + 8, :], o[:, :, :, 0:DK],
                                                    den.unsqueeze(3).broadcast_to([128, 2, 8, DK]), ALU.mult
                                                    ).then_inc(onorm_ready, 1)
                    b = st.batch(slot, T_LN2_STATS)
                    if b:
                        dve.wait_ge(y_ready, b.count(1, 1))
                        stats_of(1, b, y[b.two])
                    b = st.batch(slot, T_LN3_STATS)
                    if b:
                        dve.wait_ge(x1_ready, b.count(1, 1))
                        stats_of(2, b, x1[b.four])
                    b = st.batch(slot, T_LN3_NORM)
                    if b:
                        dve.wait_ge(rstd_step[2], b.count(2, 2))
                        if b.has(2):
                            dve.wait_ge(x1T_ps, b.count(1, -1))
                        normalise(2, b, x1n[b.two], x1[b.four], x1n_ready)
                    b = st.batch(slot, T_TREE)
                    if b:
                        U, L = u[b.two], tree[b.two]
                        dve.wait_ge(u_ready, b.count(1, 1))
                        if b.has(2):
                            dve.wait_ge(lpT_ps, b.count(1, -1))
                        nc.vector.tensor_scalar(L[:, :, 2:3], U[:, :, 0:1], -1.0, 1.0, ALU.mult, ALU.add
                                                ).then_inc(tree_step, 1)
                        nc.vector.tensor_scalar(L[:, :, 3:4], U[:, :, 0:1], 1.0, None, ALU.add).then_inc(tree_step, 1)
                        for k in range(1, LEVELS - 1):
                            n = 2**k
                            dve.wait_ge(tree_step, b.count(TREE, 2 * k))
                            nc.vector.scalar_tensor_tensor(
                                out=L[:, :, 2 * n:4 * n:2], in0=U[:, :, n - 1:2 * n - 1], scalar=1.0,
                                in1=L[:, :, n:2 * n], op0=ALU.subtract, op1=ALU.mult, reverse0=True
                            ).then_inc(tree_step, 1)
                            nc.vector.scalar_tensor_tensor(
                                out=L[:, :, 2 * n + 1:4 * n:2], in0=U[:, :, n - 1:2 * n - 1], scalar=1.0,
                                in1=L[:, :, n:2 * n], op0=ALU.add, op1=ALU.mult).then_inc(tree_step, 1)
                        dve.wait_ge(tree_step, b.count(TREE, TREE - 1))
                        nc.vector.scalar_tensor_tensor(
                            out=right[b.two][:, :, :], in0=U[:, :, HALF - 1:NODES], scalar=1.0,
                            in1=L[:, :, HALF:2 * HALF], op0=ALU.add, op1=ALU.mult).then_inc(tree_step, 1)
                    b = st.batch(slot, T_LN4_STATS)
                    if b:
                        dve.wait_ge(ret_ready, b.count(1, 1))
                        stats_of(3, b, ret[b.two])
                    for n in range(UNITS):
                        b = st.batch(slot, T_MAX + n)
                        if b:
                            g, kind = n // 3, n % 3
                            if b.has(2):
                                dve.wait_ge(m_ps, b.count(1, -1))
                            dve.wait_ge(smax_ps, b.count(UNITS, n + 1))
                            if kind == 0:
                                nc.vector.tensor_reduce(mx[b.two][:, 4 * g:4 * g + 4, 0],
                                                        smax[n % 2][:, :].rearrange("p (h t) -> p h t", h=4),
                                                        AX_X, ALU.max).then_inc(max_done, 1)
                            else:
                                h = 4 * g + 2 * (kind - 1)
                                nc.vector.tensor_reduce(mx[b.two][:, h:h + 2, 1],
                                                        smax[n % 2][:, :].rearrange("p (h t) -> p h t", h=2),
                                                        AX_X, ALU.max).then_inc(max_done, 1)

        @block.tensor
        def _(pe):
            def mm(dst, lhsT, rhs, start, stop):
                return nc.tensor.matmul(dst, lhsT, rhs, start=start, stop=stop, skip_group_check=True)

            pe.wait_ge(const_ready, 6)
            pe.wait_ge(w_loaded, 160)
            for j in range(4):
                last = nc.tensor.transpose(misc[0][:, 128 * j:128 * j + 128], wraw[:, j, :], ident[:, :])
            last.then_inc(w_turned, 1)
            for j, w in enumerate((W_R0, W_L0, W_L1, W_OUT)):
                last = nc.tensor.transpose(misc[1][:, 128 * j:128 * j + 128], wraw[:, w, :], ident[:, :])
            last.then_inc(w_turned, 1)
            nc.tensor.transpose(smax[0][:, 0:127], rraw[:, :], ident[0:127, 0:127]).then_inc(w_turned, 1)
            pe.wait_ge(w_copied, 8)
            mm(smax[1][:, 0:NODES], wraw[:, W_FQ, :], rT[:, 0:NODES], True, True).then_inc(w_fused, 1)
            leaves = wT[:, W_L0:W_L1 + 1, :].rearrange("p a n -> p (a n)")
            mm(sexp[0][:, 0:128], leaves[:, 0::2], wT[:, W_OUT, :], True, True)
            mm(sexp[0][:, 128:256], leaves[:, 1::2], wT[:, W_OUT, :], True, True).then_inc(w_fused, 1)
            pe.wait_ge(w_ready, 2)
            pe.wait_ge(buffers_set, 1)
            pe.wait_ge(bias_placed, 16)

            def causal_mask(dst, heads):
                mm(dst, identb[:, :], mask[:, :].unsqueeze(1).broadcast_to([128, heads, 128]), True, False)

            misc_read = {J_XT: (xT_ready, 1, 1), J_QK: (rest_ready, 1, 1), J_V: (v_ready, 1, 1), J_M: (m_step, 4, 2),
                         J_O[0]: (onorm_ready, 2, 1), J_O[1]: (onorm_ready, 2, 2), J_OT: (oT_ready, 1, 1),
                         J_Y: (y_ready, 1, 1), J_X1T: (x1T_ready, 1, 1), J_Z: (u_ready, 1, 1),
                         J_LPT: (lpT_ready, 1, 1), J_RET: (ret_ready, 1, 1)}

            for st in steps(pe):
                for slot in range(SLOTS):
                    bank = misc[slot % 2]
                    if any(st.batch(slot, t) for t in MISC_JOBS):
                        for before in range(slot - 2, slot - SLOTS - 1, -2):
                            t = next(t for t in MISC_JOBS if (t - before) % SLOTS == 0)
                            b = st.batch(before, t)
                            if b:
                                read, per, plus = misc_read[t]
                                pe.wait_ge(read, b.count(per, plus))
                                break

                    b = st.batch(slot, J_XT)
                    if b:
                        pe.wait_ge(xn_ready, b.count(2, 2))
                        for t in range(2):
                            last = nc.tensor.transpose(bank[:, 128 * t:128 * t + 128], xn[b.two][:, t, :], ident[:, :])
                        last.then_inc(xT_ps, 1)
                    b = st.batch(slot, J_QK)
                    if b:
                        pe.wait_ge(xT_ready, b.count(1, 1))
                        for j in range(2):
                            last = mm(bank[:, 256 * j:256 * j + 256], wqk[:, j, :], xT[b.two][:, :], True, True)
                        last.then_inc(qk_ps, 1)
                    b = st.batch(slot, J_V)
                    if b:
                        for t in range(2):
                            last = mm(bank[:, 128 * t:128 * t + 128], xT[b.two][:, 128 * t:128 * t + 128],
                                      wT[:, W_V, :], True, True)
                        last.then_inc(v_ps, 1)
                    b = st.batch(slot, J_M)
                    if b:
                        pe.wait_ge(max_done, b.count(UNITS, UNITS))
                        nc.tensor.transpose(bank[0:32, 0:128], mx[b.two][:, :, :].rearrange("p h t -> p (h t)"),
                                            ident[:, :]).then_inc(m_ps, 1)
                    for x in range(2):
                        b = st.batch(slot, J_O[x])
                        if b:
                            pe.wait_ge(oraw_ready, b.count(2, x + 1))
                            for t in range(2):
                                for g in range(2):
                                    last = nc.tensor.transpose(bank[:, 256 * t + 128 * g:256 * t + 128 * g + 128],
                                                               oraw[b.two][:, x, 256 * g + 128 * t:256 * g + 128 * t + 128],
                                                               ident[:, :])
                            last.then_inc(o_ps, 1)
                    b = st.batch(slot, J_OT)
                    if b:
                        pe.wait_ge(onorm_ready, b.count(2, 2))
                        for t in range(2):
                            last = nc.tensor.transpose(bank[:, 128 * t:128 * t + 128],
                                                       onorm[b.two][:, t, :, :].rearrange("p h d -> p (h d)"), ident[:, :])
                        last.then_inc(oT_ps, 1)
                    b = st.batch(slot, J_Y)
                    if b:
                        pe.wait_ge(oT_ready, b.count(1, 1))
                        for t in range(2):
                            last = mm(bank[:, 128 * t:128 * t + 128], oT[b.two][:, 128 * t:128 * t + 128],
                                      wT[:, W_O, :], True, True)
                        last.then_inc(y_ps, 1)
                    b = st.batch(slot, J_X1T)
                    if b:
                        pe.wait_ge(x1n_ready, b.count(2, 2))
                        for t in range(2):
                            last = nc.tensor.transpose(bank[:, 128 * t:128 * t + 128], x1n[b.two][:, t, :], ident[:, :])
                        last.then_inc(x1T_ps, 1)
                    b = st.batch(slot, J_Z)
                    if b:
                        pe.wait_ge(x1T_ready, b.count(1, 1))
                        for t in range(2):
                            last = mm(bank[:, GATES * t:GATES * t + GATES], x1T[b.two][:, 128 * t:128 * t + 128],
                                      wg[:, :], True, True)
                        last.then_inc(z_ps, 1)
                    b = st.batch(slot, J_LPT)
                    if b:
                        pe.wait_ge(tree_step, b.count(TREE, TREE))
                        for t in range(2):
                            nc.tensor.transpose(bank[:, 256 * t:256 * t + 128], tree[b.two][:, t, HALF:2 * HALF], ident[:, :])
                            last = nc.tensor.transpose(bank[:, 256 * t + 128:256 * t + 256], right[b.two][:, t, :], ident[:, :])
                        last.then_inc(lpT_ps, 1)
                    b = st.batch(slot, J_RET)
                    if b:
                        pe.wait_ge(lpT_ready, b.count(1, 1))
                        mm(bank[:, 0:256], onesb[:, :], biasb[:, :].unsqueeze(1).broadcast_to([128, 2, 128]), True, False)
                        for t in range(2):
                            mm(bank[:, 128 * t:128 * t + 128], lpT[b.two][:, t, 0, :], lva[:, :], False, False)
                            last = mm(bank[:, 128 * t:128 * t + 128], lpT[b.two][:, t, 1, :], lvb[:, :], False, True)
                        last.then_inc(ret_ps, 1)

                    for n in range(UNITS):
                        b = st.batch(slot, T_EXP + n)
                        if b:
                            g, kind = n // 3, n % 3
                            if n == 0:
                                pe.wait_ge(mrows_in[b.two], b.turns_of(2, 48))
                            if n >= 2 or b.has(1):
                                pe.wait_ge(exp_done, b.count(UNITS, n - 1))
                            S, Q, K = sexp[n % 2], qs[b.four], kd[b.four]
                            if kind < 2:
                                hp = 2 * g + kind
                                last = mm(S[:, :], K[0:STACK + MROWS, hp, 0:128],
                                          Q[0:STACK + MROWS, hp, :, :].rearrange("p s t -> p (s t)"), True, True)
                            else:
                                for j in range(2):
                                    hp = 2 * g + j
                                    last = mm(S[:, 256 * j:256 * j + 256], K[0:STACK + MROWS, hp, 128:256],
                                              Q[0:STACK + MROWS, hp, :, 128:256], True, True)
                            last.then_inc(sexp_ps, 1)
                    for n in range(UNITS):
                        b = st.batch(slot, T_MAX + n)
                        if b:
                            g, kind = n // 3, n % 3
                            if n == 0:
                                pe.wait_ge(stacked[b.four], b.turns_of(4, 16 * 12))
                            if n >= 2 or b.has(1):
                                pe.wait_ge(max_done, b.count(UNITS, n - 1))
                            S, Q, K = smax[n % 2], qs[b.four], kd[b.four]
                            if kind == 0:
                                causal_mask(S[:, :], 4)
                                for j in range(4):
                                    hp, ab = 2 * g + j // 2, j % 2
                                    last = mm(S[:, 128 * j:128 * j + 128], Q[0:STACK, hp, ab, 0:128],
                                              K[0:STACK, hp, 0:128], False, True)
                            else:
                                hp = 2 * g + kind - 1
                                causal_mask(S[:, :].rearrange("p (h t) -> p h t", h=2)[:, :, 128:256], 2)
                                for ab in range(2):
                                    last = mm(S[:, 256 * ab:256 * ab + 256], Q[0:STACK, hp, ab, 128:256],
                                              K[0:STACK, hp, :], False, True)
                            last.then_inc(smax_ps, 1)
                    for g in range(4):
                        b = st.batch(slot, T_PV + 3 * g)
                        if b:
                            pe.wait_ge(causal_done, b.count(8, 2 * g + 2))
                            if g == 0:
                                pe.wait_ge(v_ready, b.count(1, 1))
                            if g % 2 == 0 and b.has(1):
                                pe.wait_ge(oraw_ready, b.count(2, g // 2 - 1))
                            P, V, c = probs[b.two], vaug[b.four], 256 * (g % 2)
                            O = pvps[g // 2]
                            for q in range(4):
                                mm(O[32 * q:32 * q + 32, c:c + 256], V[:, 0, 4 * g + q, :],
                                   P[:, 3 * g + q // 2, 256 * (q % 2):256 * (q % 2) + 256], True, False)
                            for q in range(4):
                                last = mm(O[32 * q:32 * q + 32, c + 128:c + 256], V[:, 1, 4 * g + q, :],
                                          P[:, 3 * g + 2, 128 * q:128 * q + 128], False, True)
                            last.then_inc(pv_ps, 1)


_INS = ['L0_attn_x', 'L0_attn_w_qkv', 'L0_attn_w_o', 'L0_ffn_Wq', 'L0_ffn_routers', 'L0_ffn_leaf_keys',
        'L0_ffn_leaf_values', 'L0_ffn_Wout_w', 'L0_ffn_Wout_b']
_OUTS = [((BATCHES, SEQ, D), 'float32')]


def kernel(**inputs):
    import numpy as _np
    import concourse.bacc as _bacc
    from concourse import mybir as _mybir
    from concourse.bass_utils import run_bass_kernel_spmd as _run

    nc = _bacc.Bacc("TRN2", target_bir_lowering=False, num_devices=1)
    arrays, args = {}, []
    for name in _INS:
        a = _np.ascontiguousarray(inputs[name])
        arrays[f"in_{name}_dram"] = a
        args.append(nc.dram_tensor(f"in_{name}_dram", a.shape, _mybir.dt.from_np(a.dtype), kind="ExternalInput").ap())
    for i, (shape, dtype) in enumerate(_OUTS):
        dt = _mybir.dt.from_np(_np.dtype(dtype))
        args.append(nc.dram_tensor(f"out_{i}_dram", shape, dt, kind="ExternalOutput").ap())
    sandwich_kernel(nc, *args)
    r = _run(nc, [arrays], core_ids=[0])
    got = tuple(r.results[0][f"out_{i}_dram"] for i in range(len(_OUTS)))
    return got[0]
```

```python
from contextlib import ExitStack

import numpy as np

import concourse.bass as bass
from concourse import mybir

ALU = mybir.AluOpType
ACT = mybir.ActivationFunctionType
AX_X = mybir.AxisListType.X
F32 = mybir.dt.float32
BF16 = mybir.dt.bfloat16

BATCHES, SEQ, D = 32, 256, 128
HEADS, DK = 16, 8
TILE = 128
PAIRS = HEADS // 2
LEVELS = 8
NODES = 2**LEVELS - 1
GATES = NODES + 1
HALF = 2 ** (LEVELS - 1)
EPS = 1e-5
MASKED = -3.0e38
PARTS = ((0, 0), (1, 0), (2, 0), (0, 1), (1, 1), (0, 2))
STACK = len(PARTS) * 2 * DK
MROWS = 3
BANK = 512
UNITS = 12
SLOTS = 12
TURN = 4

T_LOAD = 0
T_LN1_STATS, T_LN1_NORM = 7, 10
J_XT = 12
J_QK, T_QK_REST, T_QK_LOW, T_STACK = 14, 15, 16, 18
J_V = 15
T_MAX = 27
J_M, T_MROWS = 40, 41
T_EXP = 46
T_CAUSAL0, T_CAUSAL1 = 47, 48
T_PV = 51
T_RELOAD = 60
J_O = (58, 65)
J_OT, J_Y = 67, 69
T_LN2_STATS, T_LN2_NORM, T_X1 = 70, 71, 72
T_LN3_STATS, T_LN3_NORM = 74, 76
J_X1T, J_Z = 78, 80
T_TREE = 81
J_LPT, J_RET = 85, 95
T_LN4_STATS, T_LN4_NORM, T_OUT, T_STORE = 96, 98, 99, 100
MISC_JOBS = (J_XT, J_QK, J_V, J_M, J_O[0], J_O[1], J_OT, J_Y, J_X1T, J_Z, J_LPT, J_RET)
LAST = T_STORE // SLOTS
ITERATIONS = BATCHES + LAST
LOOP_FROM, LOOP_TO = 8, 32
assert LOOP_FROM >= LAST and LOOP_TO <= BATCHES and LOOP_FROM % TURN == 0 and LOOP_TO % TURN == 0
assert sorted(t % SLOTS for t in MISC_JOBS) == list(range(SLOTS))


class Batch:

    def __init__(self, turn, at):
        self.turn, self.at = turn, at
        self.least = (turn if isinstance(turn, int) else LOOP_FROM // TURN) * TURN + at
        self.index = turn * TURN + at
        self.live = 0 <= self.least < BATCHES
        self.two, self.four = at % 2, at % 4

    def has(self, back):
        return self.least >= back

    def count(self, per, plus):
        return self.turn * (TURN * per) + (self.at * per + plus)

    def turns_of(self, ring, per, back=0):
        return self.turn * (TURN // ring * per) + ((self.at - back) // ring + 1) * per


class Step:

    def __init__(self, turn, at):
        self.turn, self.at = turn, at
        self.least = (turn if isinstance(turn, int) else LOOP_FROM // TURN) * TURN + at

    def batch(self, slot, time):
        if (time - slot) % SLOTS:
            return None
        b = Batch(self.turn, self.at - (time - slot) // SLOTS)
        return b if b.live else None


def steps(eng):
    for i in range(LOOP_FROM):
        yield Step(i // TURN, i % TURN)
    with eng.Fori(LOOP_FROM // TURN, LOOP_TO // TURN) as turn:
        for u in range(TURN):
            yield Step(turn, u)
    for i in range(LOOP_TO, ITERATIONS):
        yield Step(i // TURN, i % TURN)


def sandwich_kernel(nc, x, w_qkv, w_o, Wq, routers, leaf_keys, leaf_values, Wout_w, Wout_b, out):
    x_v = x.rearrange("b (t p) d -> b p t d", p=TILE)
    out_v = out.rearrange("b (t p) d -> b p t d", p=TILE)

    with ExitStack() as ctx:
        def sb(name, shape, dt=F32):
            return ctx.enter_context(nc.sbuf_tensor(name, shape, dt))

        def sem(name):
            return ctx.enter_context(nc.semaphore(name))

        misc = [ctx.enter_context(nc.psum_tensor(f"misc{i}", [128, BANK], F32)) for i in range(2)]
        smax = [ctx.enter_context(nc.psum_tensor(f"smax{i}", [128, BANK], F32)) for i in range(2)]
        sexp = [ctx.enter_context(nc.psum_tensor(f"sexp{i}", [128, BANK], F32)) for i in range(2)]
        pvps = [ctx.enter_context(nc.psum_tensor(f"pvps{i}", [128, BANK], F32)) for i in range(2)]

        ident = sb("ident", [128, 128])
        identb = sb("identb", [128, 128], BF16)
        mask = sb("mask", [128, 128], BF16)
        onesb = sb("onesb", [128, 128], BF16)
        neghalf = sb("neghalf", [128, 2])
        eps = sb("eps", [128, 2])
        zero2 = sb("zero2", [128, 2])
        wraw = sb("wraw", [128, 9, 128])
        wT = sb("wT", [128, 9, 128])
        rraw = sb("rraw", [127, 128])
        rT = sb("rT", [128, GATES])
        wqk = sb("wqk", [128, 2, 128])
        wg = sb("wg", [128, GATES])
        lva = sb("lva", [128, 128])
        lvb = sb("lvb", [128, 128])
        lvd = sb("lvd", [128, 3, 128])
        woc = sb("woc", [128, 128])
        cstats = sb("cstats", [128, 4, 6])
        cmean = sb("cmean", [128, 4, 2])
        bias_c = sb("bias_c", [1, 128])
        bias0 = sb("bias0", [1, 128])
        bias_r = sb("bias_r", [1, 2, 128])
        bias_p = sb("bias_p", [1, 3, 128], BF16)
        biasb = sb("biasb", [128, 128], BF16)

        xin = [sb(f"xin{i}", [128, 2, 128]) for i in range(2)]
        xn = [sb(f"xn{i}", [128, 2, 128]) for i in range(2)]
        xT = [sb(f"xT{i}", [128, 256]) for i in range(2)]
        parts = [sb(f"parts{i}", [128, 6, 256], BF16) for i in range(2)]
        rest = [sb(f"rest{i}", [128, 2, 256]) for i in range(2)]
        qsec = [sb(f"qsec{i}", [128, 3, 2, 256], BF16) for i in range(2)]
        qs = [sb(f"qs{i}", [128, PAIRS, 2, 256], BF16) for i in range(4)]
        kd = [sb(f"kd{i}", [128, PAIRS, 256], BF16) for i in range(4)]
        vaug = [sb(f"vaug{i}", [128, 2, HEADS, 32]) for i in range(4)]
        mx = [sb(f"mx{i}", [128, HEADS, 2]) for i in range(2)]
        mrest = [sb(f"mrest{i}", [32, 128]) for i in range(2)]
        mparts = [sb(f"mparts{i}", [32, 3, 128], BF16) for i in range(2)]
        probs = [sb(f"probs{i}", [128, UNITS, BANK]) for i in range(2)]
        oraw = [sb(f"oraw{i}", [128, 2, BANK]) for i in range(2)]
        rden = [sb(f"rden{i}", [128, 2, HEADS]) for i in range(2)]
        onorm = [sb(f"onorm{i}", [128, 2, HEADS, DK]) for i in range(2)]
        oT = [sb(f"oT{i}", [128, 256]) for i in range(2)]
        y = [sb(f"y{i}", [128, 2, 128]) for i in range(2)]
        yn = [sb(f"yn{i}", [128, 2, 128]) for i in range(2)]
        xres = [sb(f"xres{i}", [128, 2, 128]) for i in range(2)]
        x1 = [sb(f"x1{i}", [128, 2, 128]) for i in range(4)]
        x1n = [sb(f"x1n{i}", [128, 2, 128]) for i in range(2)]
        x1T = [sb(f"x1T{i}", [128, 256]) for i in range(2)]
        u = [sb(f"u{i}", [128, 2, GATES]) for i in range(2)]
        tree = [sb(f"tree{i}", [128, 2, 256]) for i in range(2)]
        right = [sb(f"right{i}", [128, 2, HALF]) for i in range(2)]
        lpT = [sb(f"lpT{i}", [128, 2, 2, 128]) for i in range(2)]
        ret = [sb(f"ret{i}", [128, 2, 128]) for i in range(2)]
        retn = [sb(f"retn{i}", [128, 2, 128]) for i in range(2)]
        outb = [sb(f"outb{i}", [128, 2, 128]) for i in range(2)]
        stats = [[sb(f"stats{k}_{i}", [128, 2, 6]) for i in range(2)] for k in range(4)]
        mv = [[sb(f"mv{k}_{i}", [128, 2, 2]) for i in range(2)] for k in range(4)]
        vare = [[sb(f"vare{k}_{i}", [128, 2]) for i in range(2)] for k in range(4)]
        rstd = [[sb(f"rstd{k}_{i}", [128, 2]) for i in range(2)] for k in range(4)]
        msq = [[sb(f"msq{k}_{i}", [128, 2]) for i in range(2)] for k in range(4)]
        square = sb("square", [128, 2, 128])
        mr = [[sb(f"mr{k}_{i}", [128, 2]) for i in range(2)] for k in range(4)]
        nmr = [[sb(f"nmr{k}_{i}", [128, 2]) for i in range(2)] for k in range(4)]

        w_loaded = sem("w_loaded")
        bias_loaded = sem("bias_loaded")
        bias_placed = sem("bias_placed")
        zeroed = sem("zeroed")
        const_ready = sem("const_ready")
        vset = sem("vset")
        w_turned = sem("w_turned")
        w_copied = sem("w_copied")
        w_fused = sem("w_fused")
        lv_step = sem("lv_step")
        centre_step = sem("centre_step")
        w_ready = sem("w_ready")
        bias_step = sem("bias_step")
        buffers_set = sem("buffers_set")

        x_loaded = [sem(f"x_loaded{i}") for i in range(2)]
        xres_loaded = [sem(f"xres_loaded{i}") for i in range(2)]
        stacked = [sem(f"stacked{i}") for i in range(4)]
        mrows_in = [sem(f"mrows_in{i}") for i in range(2)]
        stored = [sem(f"stored{i}") for i in range(2)]
        stats_done = [sem(f"stats_done{k}") for k in range(4)]
        mv_ready = [sem(f"mv_ready{k}") for k in range(4)]
        rstd_step = [sem(f"rstd_step{k}") for k in range(4)]
        xn_ready = sem("xn_ready")
        xT_ps = sem("xT_ps")
        xT_ready = sem("xT_ready")
        qk_ps = sem("qk_ps")
        v_ps = sem("v_ps")
        hi_ready = sem("hi_ready")
        rest_ready = sem("rest_ready")
        mid_ready = sem("mid_ready")
        lo_ready = sem("lo_ready")
        qsec_ready = sem("qsec_ready")
        v_ready = sem("v_ready")
        smax_ps = sem("smax_ps")
        max_done = sem("max_done")
        m_ps = sem("m_ps")
        m_step = sem("m_step")
        sexp_ps = sem("sexp_ps")
        exp_done = sem("exp_done")
        causal_done = sem("causal_done")
        pv_ps = sem("pv_ps")
        oraw_ready = sem("oraw_ready")
        o_ps = sem("o_ps")
        rden_ready = sem("rden_ready")
        onorm_ready = sem("onorm_ready")
        oT_ps = sem("oT_ps")
        oT_ready = sem("oT_ready")
        y_ps = sem("y_ps")
        y_ready = sem("y_ready")
        yn_ready = sem("yn_ready")
        x1_ready = sem("x1_ready")
        x1n_ready = sem("x1n_ready")
        x1T_ps = sem("x1T_ps")
        x1T_ready = sem("x1T_ready")
        z_ps = sem("z_ps")
        u_ready = sem("u_ready")
        tree_step = sem("tree_step")
        lpT_ps = sem("lpT_ps")
        lpT_ready = sem("lpT_ready")
        ret_ps = sem("ret_ps")
        ret_ready = sem("ret_ready")
        retn_ready = sem("retn_ready")
        out_ready = sem("out_ready")
        TREE = 2 * (LEVELS - 1) + 1

        w_src = [w_qkv[i].rearrange("h k m -> (h k) m") for i in range(3)] + [
            w_o, Wout_w, Wq, routers[0:128, :], leaf_values[0:128, :], leaf_values[128:256, :]]
        W_Q, W_K, W_V, W_O, W_OUT, W_FQ, W_R0, W_L0, W_L1 = range(9)

        block = ctx.enter_context(nc.Block())

        @block.sync
        def _(sp):
            for j, src in enumerate(w_src):
                sp.dma_start(wraw[:, j, :], src).then_inc(w_loaded, 16)
            sp.dma_start(rraw[:, :], routers[128:NODES, :]).then_inc(w_loaded, 16)
            sp.dma_start(bias0[:, :], Wout_b.rearrange("(a d) -> a d", a=1)).then_inc(bias_loaded, 16)
            sp.wait_ge(bias_step, 5)
            sp.dma_start(biasb[0:3, :], bias_p[:, :, :]).then_inc(bias_placed, 16)

            for st in steps(sp):
                for slot in range(SLOTS):
                    b = st.batch(slot, T_LOAD)
                    if b:
                        if b.has(2):
                            sp.wait_ge(xn_ready, b.count(2, -2))
                        sp.dma_start(xin[b.two][:, :, :], x_v[b.index]).then_inc(x_loaded[b.two], 16)
                    b = st.batch(slot, T_STACK)
                    if b:
                        if b.has(4):
                            sp.wait_ge(sexp_ps, b.count(UNITS, -3 * UNITS))
                        for j, (_, part) in enumerate(PARTS):
                            if part == 0:
                                sp.wait_ge(hi_ready, b.count(1, 1))
                            elif part == 1:
                                sp.wait_ge(mid_ready, b.count(1, 1))
                            else:
                                sp.wait_ge(lo_ready, b.count(1, 1))
                            sp.dma_start(kd[b.four][16 * j:16 * j + 16, :, :],
                                         parts[b.two][:, 5 - part, :]).then_inc(stacked[b.four], 16)
                        sp.wait_ge(qsec_ready, b.count(2, 2))
                        for j, (part, _) in enumerate(PARTS):
                            sp.dma_start(qs[b.four][16 * j:16 * j + 16, :, :, :].rearrange("p h s t -> p h (s t)"),
                                         qsec[b.two][:, part, :, :].rearrange("p s t -> p (s t)")
                                         ).then_inc(stacked[b.four], 16)
                    b = st.batch(slot, T_MROWS)
                    if b:
                        sp.wait_ge(m_step, b.count(4, 4))
                        for j in range(MROWS):
                            sp.dma_start(qs[b.four][STACK + j:STACK + j + 1, :, :, :].rearrange("p h s t -> p (h s t)"),
                                         mparts[b.two][:, j, :]).then_inc(mrows_in[b.two], 16)
                    b = st.batch(slot, T_RELOAD)
                    if b:
                        if b.has(2):
                            sp.wait_ge(x1_ready, b.count(1, -1))
                        sp.dma_start(xres[b.two][:, :, :], x_v[b.index]).then_inc(xres_loaded[b.two], 16)
                    b = st.batch(slot, T_STORE)
                    if b:
                        sp.wait_ge(out_ready, b.count(1, 1))
                        sp.dma_start(out_v[b.index], outb[b.two][:, :, :]).then_inc(stored[b.two], 16)
            for i in range(2):
                sp.wait_ge(stored[i], 16 * (BATCHES // 2))

        @block.gpsimd
        def _(pool):
            nc.gpsimd.memset(ident[:, :], 0.0).then_inc(zeroed, 1)
            nc.gpsimd.memset(identb[:, :], 0.0).then_inc(zeroed, 1)
            nc.gpsimd.memset(mask[:, :], 0.0).then_inc(zeroed, 1)
            nc.gpsimd.memset(onesb[:, :], 0.0).then_inc(zeroed, 1)
            nc.gpsimd.memset(neghalf[:, :], -0.5).then_inc(const_ready, 1)
            nc.gpsimd.memset(eps[:, :], EPS).then_inc(zeroed, 1)
            nc.gpsimd.memset(zero2[:, :], 0.0).then_inc(const_ready, 1)
            pool.wait_ge(zeroed, 5)
            nc.gpsimd.affine_select(out=ident[:, :], in_=ident[:, :], compare_op=ALU.not_equal, fill=1.0,
                                    base=0, pattern=[[-1, 128]], channel_multiplier=1).then_inc(const_ready, 1)
            nc.gpsimd.affine_select(out=identb[:, :], in_=identb[:, :], compare_op=ALU.not_equal, fill=1.0,
                                    base=0, pattern=[[-1, 128]], channel_multiplier=1).then_inc(const_ready, 1)
            nc.gpsimd.affine_select(out=mask[:, :], in_=mask[:, :], compare_op=ALU.is_ge, fill=MASKED,
                                    base=0, pattern=[[-1, 128]], channel_multiplier=1).then_inc(const_ready, 1)
            nc.gpsimd.affine_select(out=onesb[:, :], in_=onesb[:, :], compare_op=ALU.is_ge, fill=1.0,
                                    base=-3, pattern=[[0, 128]], channel_multiplier=1).then_inc(const_ready, 1)

            def rstd_of(k, b):
                two, step = b.two, rstd_step[k]
                steps_each = 4 if k == 0 else 2
                pool.wait_ge(mv_ready[k], b.count(2, 2))
                variance = msq[k][two][:, :] if k in (1, 3) else mv[k][two][:, :, 1]
                nc.gpsimd.tensor_tensor(vare[k][two][:, :], variance, eps[:, :],
                                        ALU.add).then_inc(step, 1)
                pool.wait_ge(step, b.count(steps_each, 1))
                nc.gpsimd.tensor_tensor(rstd[k][two][:, :], vare[k][two][:, :], neghalf[:, :],
                                        ALU.pow).then_inc(step, 1)
                if k == 0:
                    pool.wait_ge(step, b.count(4, 2))
                    nc.gpsimd.tensor_tensor(mr[k][two][:, :], mv[k][two][:, :, 0], rstd[k][two][:, :],
                                            ALU.mult).then_inc(step, 1)
                    pool.wait_ge(step, b.count(4, 3))
                    nc.gpsimd.tensor_tensor(nmr[k][two][:, :], zero2[:, :], mr[k][two][:, :],
                                            ALU.subtract).then_inc(step, 1)

            def causal(b, units, view):
                pool.wait_ge(exp_done, b.count(UNITS, units))
                pool.nop(nofuse=True)
                nc.gpsimd.affine_select(out=view, in_=view, compare_op=ALU.is_ge, fill=0.0, base=0,
                                        pattern=[[0, 4], [1, 128]], channel_multiplier=-1
                                        ).then_inc(causal_done, 1)

            for st in steps(pool):
                for slot in range(SLOTS):
                    b = st.batch(slot, T_LN1_STATS)
                    if b:
                        rstd_of(0, b)
                    b = st.batch(slot, T_QK_LOW)
                    if b:
                        pool.wait_ge(mid_ready, b.count(1, 1))
                        nc.gpsimd.tensor_tensor(parts[b.two][:, 2:4, :], rest[b.two][:, :, :],
                                                parts[b.two][:, 1:5:3, :], ALU.subtract).then_inc(lo_ready, 1)
                    for g in range(4):
                        b = st.batch(slot, T_CAUSAL0 + 3 * g)
                        if b:
                            causal(b, 3 * g + 2, probs[b.two][:, 3 * g:3 * g + 2, :].rearrange(
                                "p u (h s) -> p (u h) s", h=2)[:, :, 0:128])
                        b = st.batch(slot, T_CAUSAL1 + 3 * g)
                        if b:
                            causal(b, 3 * g + 3, probs[b.two][:, 3 * g + 2, :].rearrange(
                                "p (h s) -> p h s", h=4))
                    b = st.batch(slot, T_LN2_STATS)
                    if b:
                        rstd_of(1, b)
                    b = st.batch(slot, T_X1)
                    if b:
                        pool.wait_ge(yn_ready, b.count(2, 2))
                        pool.wait_ge(xres_loaded[b.two], b.turns_of(2, 16))
                        nc.gpsimd.tensor_tensor(x1[b.four][:, :, :], xres[b.two][:, :, :], yn[b.two][:, :, :],
                                                ALU.add).then_inc(x1_ready, 1)
                    b = st.batch(slot, T_LN3_STATS)
                    if b:
                        rstd_of(2, b)
                    b = st.batch(slot, T_LN4_STATS)
                    if b:
                        rstd_of(3, b)
                    b = st.batch(slot, T_OUT)
                    if b:
                        pool.wait_ge(retn_ready, b.count(2, 2))
                        if b.has(2):
                            pool.wait_ge(stored[b.two], b.turns_of(2, 16, 2))
                        nc.gpsimd.tensor_tensor(outb[b.two][:, :, :], x1[b.four][:, :, :], retn[b.two][:, :, :],
                                                ALU.add).then_inc(out_ready, 1)

        @block.scalar
        def _(act):
            def copy(dst, src):
                return nc.scalar.activation(dst, src, ACT.Copy)

            act.wait_ge(w_turned, 1)
            copy(wT[:, W_V, :], misc[0][:, 256:384]).then_inc(w_copied, 1)
            for j in (W_Q, W_K):
                copy(wqk[:, j, :].rearrange("p (a d h) -> p a d h", a=2, d=DK),
                     misc[0][:, 128 * j:128 * j + 128].rearrange("p (h a d) -> p a d h", a=2, d=DK)
                     ).then_inc(w_copied, 1)
            copy(wT[:, W_O, :], misc[0][:, 384:512]).then_inc(w_copied, 1)
            act.wait_ge(w_turned, 2)
            copy(rT[:, 0:128], misc[1][:, 0:128]).then_inc(w_copied, 1)
            copy(wT[:, W_L0:W_L1 + 1, :].rearrange("p a n -> p (a n)"), misc[1][:, 128:384]).then_inc(w_copied, 1)
            copy(wT[:, W_OUT, :], misc[1][:, 384:512]).then_inc(w_copied, 1)
            act.wait_ge(w_turned, 3)
            copy(rT[:, 128:NODES], smax[0][:, 0:127]).then_inc(w_copied, 1)
            act.wait_ge(w_fused, 1)
            copy(wg[:, 0:NODES], smax[1][:, 0:NODES]).then_inc(w_ready, 1)

            def mean_squares(k, b, src):
                for t in range(2):
                    nc.scalar.activation(square[:, t, :], src[:, 128 * t:128 * t + 128], ACT.Square,
                                         scale=float(D) ** -0.5, accum_out=msq[k][b.two][:, t:t + 1]
                                         ).then_inc(mv_ready[k], 1)

            def scale_rows(k, b, dst, src, ready):
                for t in range(2):
                    nc.scalar.activation(dst[:, t, :], src[:, t, :], ACT.Copy, scale=rstd[k][b.two][:, t:t + 1]
                                         ).then_inc(ready, 1)

            for st in steps(act):
                for slot in range(SLOTS):
                    b = st.batch(slot, T_LN1_NORM)
                    if b:
                        act.wait_ge(rstd_step[0], b.count(4, 4))
                        if b.has(2):
                            act.wait_ge(xT_ps, b.count(1, -1))
                        for t in range(2):
                            nc.scalar.activation(xn[b.two][:, t, :], xin[b.two][:, t, :], ACT.Identity,
                                                 bias=nmr[0][b.two][:, t:t + 1], scale=rstd[0][b.two][:, t:t + 1]
                                                 ).then_inc(xn_ready, 1)
                    b = st.batch(slot, J_XT)
                    if b:
                        act.wait_ge(xT_ps, b.count(1, 1))
                        if b.has(2):
                            act.wait_ge(v_ps, b.count(1, -1))
                        copy(xT[b.two][:, :], misc[slot % 2][:, 0:256]).then_inc(xT_ready, 1)
                    b = st.batch(slot, J_QK)
                    if b:
                        act.wait_ge(qk_ps, b.count(1, 1))
                        if b.has(2):
                            act.wait_ge(stacked[(b.four + 2) % 4], b.turns_of(4, 16 * 12, 2))
                        copy(parts[b.two][:, 0::5, :], misc[slot % 2][:, :].rearrange("p (a n) -> p a n", a=2)
                             ).then_inc(hi_ready, 1)
                    b = st.batch(slot, T_QK_LOW)
                    if b:
                        act.wait_ge(rest_ready, b.count(1, 1))
                        copy(parts[b.two][:, 1:5:3, :], rest[b.two][:, :, :]).then_inc(mid_ready, 1)
                    b = st.batch(slot, J_V)
                    if b:
                        act.wait_ge(v_ps, b.count(1, 1))
                        if b.has(4):
                            act.wait_ge(pv_ps, b.count(4, -12))
                        else:
                            act.wait_ge(buffers_set, 1)
                        copy(vaug[b.four][:, :, :, 0:DK],
                             misc[slot % 2][:, 0:256].rearrange("p (t h d) -> p t h d", t=2, d=DK)
                             ).then_inc(v_ready, 1)
                    for g in (1, 3):
                        b = st.batch(slot, T_PV + 3 * g)
                        if b:
                            act.wait_ge(pv_ps, b.count(4, g + 1))
                            if b.has(2):
                                act.wait_ge(o_ps, b.count(2, -4 + g // 2 + 1))
                            copy(oraw[b.two][:, g // 2, :], pvps[g // 2][:, :]).then_inc(oraw_ready, 1)
                    b = st.batch(slot, J_OT)
                    if b:
                        act.wait_ge(oT_ps, b.count(1, 1))
                        if b.has(2):
                            act.wait_ge(y_ps, b.count(1, -1))
                        copy(oT[b.two][:, :], misc[slot % 2][:, 0:256]).then_inc(oT_ready, 1)
                    b = st.batch(slot, J_Y)
                    if b:
                        act.wait_ge(y_ps, b.count(1, 1))
                        mean_squares(1, b, misc[slot % 2])
                        copy(y[b.two][:, :, :].rearrange("p t n -> p (t n)"), misc[slot % 2][:, 0:256]
                             ).then_inc(y_ready, 1)
                    b = st.batch(slot, T_LN2_NORM)
                    if b:
                        act.wait_ge(rstd_step[1], b.count(2, 2))
                        if b.has(2):
                            act.wait_ge(x1_ready, b.count(1, -1))
                        act.wait_ge(y_ready, b.count(1, 1))
                        scale_rows(1, b, yn[b.two], y[b.two], yn_ready)
                    b = st.batch(slot, J_X1T)
                    if b:
                        act.wait_ge(x1T_ps, b.count(1, 1))
                        if b.has(2):
                            act.wait_ge(z_ps, b.count(1, -1))
                        copy(x1T[b.two][:, :], misc[slot % 2][:, 0:256]).then_inc(x1T_ready, 1)
                    b = st.batch(slot, J_Z)
                    if b:
                        act.wait_ge(z_ps, b.count(1, 1))
                        if b.has(2):
                            act.wait_ge(tree_step, b.count(TREE, -TREE))
                        nc.scalar.activation(u[b.two][:, :, :].rearrange("p t n -> p (t n)"), misc[slot % 2][:, :],
                                             ACT.Tanh, scale=0.5).then_inc(u_ready, 1)
                    b = st.batch(slot, J_LPT)
                    if b:
                        act.wait_ge(lpT_ps, b.count(1, 1))
                        if b.has(2):
                            act.wait_ge(ret_ps, b.count(1, -1))
                        copy(lpT[b.two][:, :, :, :].rearrange("p t a n -> p (t a n)"), misc[slot % 2][:, :]
                             ).then_inc(lpT_ready, 1)
                    b = st.batch(slot, J_RET)
                    if b:
                        act.wait_ge(ret_ps, b.count(1, 1))
                        mean_squares(3, b, misc[slot % 2])
                        copy(ret[b.two][:, :, :].rearrange("p t n -> p (t n)"), misc[slot % 2][:, 0:256]
                             ).then_inc(ret_ready, 1)
                    b = st.batch(slot, T_LN4_NORM)
                    if b:
                        act.wait_ge(rstd_step[3], b.count(2, 2))
                        if b.has(2):
                            act.wait_ge(out_ready, b.count(1, -1))
                        act.wait_ge(ret_ready, b.count(1, 1))
                        scale_rows(3, b, retn[b.two], ret[b.two], retn_ready)
                    for n in range(UNITS):
                        b = st.batch(slot, T_EXP + n)
                        if b:
                            act.wait_ge(sexp_ps, b.count(UNITS, n + 1))
                            if b.has(2):
                                act.wait_ge(pv_ps, b.count(4, -8 + n // 3 + 1))
                            nc.scalar.activation(probs[b.two][:, n, :], sexp[n % 2][:, :], ACT.Exp,
                                                 scale=float(DK) ** -0.5).then_inc(exp_done, 1)

        @block.vector
        def _(dve):
            for i in range(4):
                nc.vector.memset(vaug[i][:, :, :, :], 0.0).then_inc(vset, 1)
                nc.vector.memset(kd[i][96:128, :, :], -1.0).then_inc(vset, 1)
            for i in range(2):
                nc.vector.memset(qsec[i][:, :, :, :], 0.0).then_inc(vset, 1)
            nc.vector.memset(biasb[:, :], 0.0).then_inc(vset, 1)
            nc.vector.memset(wg[:, NODES:GATES], 0.0).then_inc(vset, 1)
            dve.wait_ge(vset, 12)
            for i in range(4):
                last = nc.vector.memset(vaug[i][:, :, :, DK:DK + 1], 1.0)
            last.then_inc(buffers_set, 1)
            centred = [0]

            def centre(dst, src, rows):
                n = centred[0]
                centred[0] += 1
                nc.vector.bn_stats(cstats[0:rows, n, :], src).then_inc(centre_step, 1)
                dve.wait_ge(centre_step, 3 * n + 1)
                nc.vector.bn_aggr(cmean[0:rows, n, :], cstats[0:rows, n, :]).then_inc(centre_step, 1)
                dve.wait_ge(centre_step, 3 * n + 2)
                nc.vector.tensor_scalar(dst, src, cmean[0:rows, n, 0:1], None, ALU.subtract).then_inc(centre_step, 1)
                dve.wait_ge(centre_step, 3 * n + 3)

            dve.wait_ge(bias_loaded, 16)
            centre(bias_c[:, :], bias0[:, :], 1)
            for j in range(3):
                src = bias_c[:, :] if j == 0 else bias_r[:, j - 1, :]
                nc.vector.tensor_copy(bias_p[:, j, :], src).then_inc(bias_step, 1)
                if j < 2:
                    dve.wait_ge(bias_step, 2 * j + 1)
                    nc.vector.tensor_tensor(bias_r[:, j, :], src, bias_p[:, j, :], ALU.subtract).then_inc(bias_step, 1)
                    dve.wait_ge(bias_step, 2 * j + 2)
            dve.wait_ge(w_copied, 4)
            centre(woc[:, :], wT[:, W_O, :], 128)
            dve.wait_ge(w_fused, 2)
            nc.vector.tensor_scalar(lvd[:, 0, :], sexp[0][:, 0:128], 0.5 ** (LEVELS - 1), None, ALU.mult).then_inc(lv_step, 1)
            nc.vector.tensor_scalar(lvd[:, 1, :], sexp[0][:, 128:256], 0.5 ** LEVELS, None, ALU.mult).then_inc(lv_step, 1)
            dve.wait_ge(lv_step, 2)
            centre(lva[:, :], lvd[:, 0, :], 128)
            centre(lvd[:, 2, :], lvd[:, 1, :], 128)
            nc.vector.scalar_tensor_tensor(out=lvb[:, :], in0=lva[:, :], scalar=-0.5, in1=lvd[:, 2, :],
                                           op0=ALU.mult, op1=ALU.add).then_inc(w_ready, 1)

            def stats_of(k, b, src):
                for t in range(2):
                    nc.vector.bn_stats(stats[k][b.two][:, t, :], src[:, t, :]).then_inc(stats_done[k], 1)

            def aggregate(k, b):
                for t in range(2):
                    dve.wait_ge(stats_done[k], b.count(2, t + 1))
                    dve.nop(nofuse=True)
                    nc.vector.bn_aggr(mv[k][b.two][:, t, :], stats[k][b.two][:, t, :]).then_inc(mv_ready[k], 1)

            def tree_level(b, k):
                U, L, n = u[b.two], tree[b.two], 2**k
                if k == 0:
                    dve.wait_ge(u_ready, b.count(1, 1))
                    if b.has(2):
                        dve.wait_ge(lpT_ps, b.count(1, -1))
                    nc.vector.tensor_scalar(L[:, :, 2:3], U[:, :, 0:1], -1.0, 1.0, ALU.mult, ALU.add
                                            ).then_inc(tree_step, 1)
                    nc.vector.tensor_scalar(L[:, :, 3:4], U[:, :, 0:1], 1.0, None, ALU.add).then_inc(tree_step, 1)
                    return
                dve.wait_ge(tree_step, b.count(TREE, 2 * k))
                if k < LEVELS - 1:
                    nc.vector.scalar_tensor_tensor(
                        out=L[:, :, 2 * n:4 * n:2], in0=U[:, :, n - 1:2 * n - 1], scalar=1.0,
                        in1=L[:, :, n:2 * n], op0=ALU.subtract, op1=ALU.mult, reverse0=True).then_inc(tree_step, 1)
                dst = L[:, :, 2 * n + 1:4 * n:2] if k < LEVELS - 1 else right[b.two][:, :, :]
                nc.vector.scalar_tensor_tensor(
                    out=dst, in0=U[:, :, n - 1:2 * n - 1], scalar=1.0,
                    in1=L[:, :, n:2 * n], op0=ALU.add, op1=ALU.mult).then_inc(tree_step, 1)

            for st in steps(dve):
                for slot in range(SLOTS):
                    b = st.batch(slot, T_LN1_STATS)
                    if b:
                        dve.wait_ge(x_loaded[b.two], b.turns_of(2, 16))
                        stats_of(0, b, xin[b.two])
                    b = st.batch(slot, T_QK_REST)
                    if b:
                        dve.wait_ge(hi_ready, b.count(1, 1))
                        if b.has(2):
                            dve.wait_ge(lo_ready, b.count(1, -1))
                        nc.vector.tensor_tensor(rest[b.two][:, :, :],
                                                misc[J_QK % 2][:, :].rearrange("p (a n) -> p a n", a=2),
                                                parts[b.two][:, 0::5, :], ALU.subtract).then_inc(rest_ready, 1)
                    b = st.batch(slot, J_M)
                    if b:
                        dve.wait_ge(m_ps, b.count(1, 1))
                        if b.has(2):
                            dve.wait_ge(mrows_in[b.two], b.turns_of(2, 48, 2))
                        nc.vector.tensor_copy(mparts[b.two][:, 0, :], misc[J_M % 2][0:32, 0:128]).then_inc(m_step, 1)
                    b = st.batch(slot, J_M + 1)
                    if b:
                        dve.wait_ge(m_step, b.count(4, 2))
                        nc.vector.tensor_copy(mparts[b.two][:, 1, :], mrest[b.two][:, :]).then_inc(m_step, 1)
                    for x in range(2):
                        b = st.batch(slot, J_O[x])
                        if b:
                            dve.wait_ge(o_ps, b.count(2, x + 1))
                            nc.vector.reciprocal(rden[b.two][:, :, 8 * x:8 * x + 8],
                                                 misc[slot % 2][:, :].rearrange("p (t h c) -> p t h c", t=2, h=8)[:, :, :, DK]
                                                 ).then_inc(rden_ready, 1)
                    b = st.batch(slot, T_LN3_STATS)
                    if b:
                        dve.wait_ge(x1_ready, b.count(1, 1))
                        stats_of(2, b, x1[b.four])
                    for k in range(0, LEVELS, 2):
                        b = st.batch(slot, T_TREE + k // 2)
                        if b:
                            tree_level(b, k)
                    for n in range(UNITS):
                        b = st.batch(slot, T_MAX + n)
                        if b:
                            g, kind = n // 3, n % 3
                            if b.has(2):
                                dve.wait_ge(m_ps, b.count(1, -1))
                            dve.wait_ge(smax_ps, b.count(UNITS, n + 1))
                            heads = 4 if kind == 0 else 2
                            h = 4 * g if kind == 0 else 4 * g + 2 * (kind - 1)
                            nc.vector.tensor_reduce(mx[b.two][:, h:h + heads, min(kind, 1)],
                                                    smax[n % 2][:, :].rearrange("p (h t) -> p h t", h=heads),
                                                    AX_X, ALU.max).then_inc(max_done, 1)
                    b = st.batch(slot, T_LN1_STATS)
                    if b:
                        aggregate(0, b)
                    b = st.batch(slot, J_M)
                    if b:
                        dve.wait_ge(m_step, b.count(4, 1))
                        nc.vector.tensor_tensor(mrest[b.two][:, :], misc[J_M % 2][0:32, 0:128], mparts[b.two][:, 0, :],
                                                ALU.subtract).then_inc(m_step, 1)
                    b = st.batch(slot, J_M + 1)
                    if b:
                        dve.wait_ge(m_step, b.count(4, 3))
                        nc.vector.tensor_tensor(mparts[b.two][:, 2, :], mrest[b.two][:, :], mparts[b.two][:, 1, :],
                                                ALU.subtract).then_inc(m_step, 1)
                    for x in range(2):
                        b = st.batch(slot, J_O[x])
                        if b:
                            dve.wait_ge(rden_ready, b.count(2, x + 1))
                            if b.has(2):
                                dve.wait_ge(oT_ps, b.count(1, -1))
                            nc.vector.tensor_tensor(onorm[b.two][:, :, 8 * x:8 * x + 8, :],
                                                    misc[slot % 2][:, :].rearrange("p (t h c) -> p t h c", t=2, h=8)[:, :, :, 0:DK],
                                                    rden[b.two][:, :, 8 * x:8 * x + 8].unsqueeze(3).broadcast_to([128, 2, 8, DK]),
                                                    ALU.mult).then_inc(onorm_ready, 1)
                    b = st.batch(slot, T_LN3_STATS)
                    if b:
                        aggregate(2, b)
                    b = st.batch(slot, T_LN3_NORM)
                    if b:
                        dve.wait_ge(rstd_step[2], b.count(2, 2))
                        if b.has(2):
                            dve.wait_ge(x1T_ps, b.count(1, -1))
                        for t in range(2):
                            nc.vector.tensor_scalar(x1n[b.two][:, t, :], x1[b.four][:, t, :], mv[2][b.two][:, t, 0:1],
                                                    rstd[2][b.two][:, t:t + 1], ALU.subtract, ALU.mult).then_inc(x1n_ready, 1)
                    for k in range(1, LEVELS, 2):
                        b = st.batch(slot, T_TREE + k // 2)
                        if b:
                            tree_level(b, k)
                    b = st.batch(slot, T_STACK)
                    if b:
                        dve.wait_ge(lo_ready, b.count(1, 1))
                        for ab in range(2):
                            rows = slice(64 * ab, 64 * ab + 64)
                            for part in range(3):
                                last = nc.vector.tensor_copy(qsec[b.two][rows, part, ab, :], parts[b.two][rows, part, :])
                            last.then_inc(qsec_ready, 1)

        @block.tensor
        def _(pe):
            def mm(dst, lhsT, rhs, start, stop):
                return nc.tensor.matmul(dst, lhsT, rhs, start=start, stop=stop, skip_group_check=True)

            pe.wait_ge(const_ready, 6)
            pe.wait_ge(w_loaded, 160)
            for j in range(4):
                last = nc.tensor.transpose(misc[0][:, 128 * j:128 * j + 128], wraw[:, j, :], ident[:, :])
            last.then_inc(w_turned, 1)
            for j, w in enumerate((W_R0, W_L0, W_L1, W_OUT)):
                last = nc.tensor.transpose(misc[1][:, 128 * j:128 * j + 128], wraw[:, w, :], ident[:, :])
            last.then_inc(w_turned, 1)
            nc.tensor.transpose(smax[0][:, 0:127], rraw[:, :], ident[0:127, 0:127]).then_inc(w_turned, 1)
            pe.wait_ge(w_copied, 8)
            mm(smax[1][:, 0:NODES], wraw[:, W_FQ, :], rT[:, 0:NODES], True, True).then_inc(w_fused, 1)
            leaves = wT[:, W_L0:W_L1 + 1, :].rearrange("p a n -> p (a n)")
            mm(sexp[0][:, 0:128], leaves[:, 0::2], wT[:, W_OUT, :], True, True)
            mm(sexp[0][:, 128:256], leaves[:, 1::2], wT[:, W_OUT, :], True, True).then_inc(w_fused, 1)
            pe.wait_ge(w_ready, 2)
            pe.wait_ge(buffers_set, 1)
            pe.wait_ge(bias_placed, 16)

            def causal_mask(dst, heads):
                mm(dst, identb[:, :], mask[:, :].unsqueeze(1).broadcast_to([128, heads, 128]), True, False)

            misc_read = {J_XT: (xT_ready, 1, 1), J_QK: (rest_ready, 1, 1), J_V: (v_ready, 1, 1), J_M: (m_step, 4, 2),
                         J_O[0]: (onorm_ready, 2, 1), J_O[1]: (onorm_ready, 2, 2), J_OT: (oT_ready, 1, 1),
                         J_Y: (y_ready, 1, 1), J_X1T: (x1T_ready, 1, 1), J_Z: (u_ready, 1, 1),
                         J_LPT: (lpT_ready, 1, 1), J_RET: (ret_ready, 1, 1)}

            for st in steps(pe):
                for slot in range(SLOTS):
                    bank = misc[slot % 2]
                    if any(st.batch(slot, t) for t in MISC_JOBS):
                        for before in range(slot - 2, slot - SLOTS - 1, -2):
                            t = next(t for t in MISC_JOBS if (t - before) % SLOTS == 0)
                            b = st.batch(before, t)
                            if b:
                                read, per, plus = misc_read[t]
                                pe.wait_ge(read, b.count(per, plus))
                                break

                    b = st.batch(slot, J_XT)
                    if b:
                        pe.wait_ge(xn_ready, b.count(2, 2))
                        for t in range(2):
                            last = nc.tensor.transpose(bank[:, 128 * t:128 * t + 128], xn[b.two][:, t, :], ident[:, :])
                        last.then_inc(xT_ps, 1)
                    b = st.batch(slot, J_QK)
                    if b:
                        pe.wait_ge(xT_ready, b.count(1, 1))
                        for j in range(2):
                            last = mm(bank[:, 256 * j:256 * j + 256], wqk[:, j, :], xT[b.two][:, :], True, True)
                        last.then_inc(qk_ps, 1)
                    b = st.batch(slot, J_V)
                    if b:
                        for t in range(2):
                            last = mm(bank[:, 128 * t:128 * t + 128], xT[b.two][:, 128 * t:128 * t + 128],
                                      wT[:, W_V, :], True, True)
                        last.then_inc(v_ps, 1)
                    b = st.batch(slot, J_M)
                    if b:
                        pe.wait_ge(max_done, b.count(UNITS, UNITS))
                        nc.tensor.transpose(bank[0:32, 0:128], mx[b.two][:, :, :].rearrange("p h t -> p (h t)"),
                                            ident[:, :]).then_inc(m_ps, 1)
                    for x in range(2):
                        b = st.batch(slot, J_O[x])
                        if b:
                            pe.wait_ge(oraw_ready, b.count(2, x + 1))
                            for t in range(2):
                                for g in range(2):
                                    last = nc.tensor.transpose(bank[:, 256 * t + 128 * g:256 * t + 128 * g + 128],
                                                               oraw[b.two][:, x, 256 * g + 128 * t:256 * g + 128 * t + 128],
                                                               ident[:, :])
                            last.then_inc(o_ps, 1)
                    b = st.batch(slot, J_OT)
                    if b:
                        pe.wait_ge(onorm_ready, b.count(2, 2))
                        for t in range(2):
                            last = nc.tensor.transpose(bank[:, 128 * t:128 * t + 128],
                                                       onorm[b.two][:, t, :, :].rearrange("p h d -> p (h d)"), ident[:, :])
                        last.then_inc(oT_ps, 1)
                    b = st.batch(slot, J_Y)
                    if b:
                        pe.wait_ge(oT_ready, b.count(1, 1))
                        for t in range(2):
                            last = mm(bank[:, 128 * t:128 * t + 128], oT[b.two][:, 128 * t:128 * t + 128],
                                      woc[:, :], True, True)
                        last.then_inc(y_ps, 1)
                    b = st.batch(slot, J_X1T)
                    if b:
                        pe.wait_ge(x1n_ready, b.count(2, 2))
                        for t in range(2):
                            last = nc.tensor.transpose(bank[:, 128 * t:128 * t + 128], x1n[b.two][:, t, :], ident[:, :])
                        last.then_inc(x1T_ps, 1)
                    b = st.batch(slot, J_Z)
                    if b:
                        pe.wait_ge(x1T_ready, b.count(1, 1))
                        for t in range(2):
                            last = mm(bank[:, GATES * t:GATES * t + GATES], x1T[b.two][:, 128 * t:128 * t + 128],
                                      wg[:, :], True, True)
                        last.then_inc(z_ps, 1)
                    b = st.batch(slot, J_LPT)
                    if b:
                        pe.wait_ge(tree_step, b.count(TREE, TREE))
                        for t in range(2):
                            nc.tensor.transpose(bank[:, 256 * t:256 * t + 128], tree[b.two][:, t, HALF:2 * HALF], ident[:, :])
                            last = nc.tensor.transpose(bank[:, 256 * t + 128:256 * t + 256], right[b.two][:, t, :], ident[:, :])
                        last.then_inc(lpT_ps, 1)
                    b = st.batch(slot, J_RET)
                    if b:
                        pe.wait_ge(lpT_ready, b.count(1, 1))
                        mm(bank[:, 0:256], onesb[:, :], biasb[:, :].unsqueeze(1).broadcast_to([128, 2, 128]), True, False)
                        for t in range(2):
                            mm(bank[:, 128 * t:128 * t + 128], lpT[b.two][:, t, 0, :], lva[:, :], False, False)
                            last = mm(bank[:, 128 * t:128 * t + 128], lpT[b.two][:, t, 1, :], lvb[:, :], False, True)
                        last.then_inc(ret_ps, 1)

                    for n in range(UNITS):
                        b = st.batch(slot, T_EXP + n)
                        if b:
                            g, kind = n // 3, n % 3
                            if n == 0:
                                pe.wait_ge(mrows_in[b.two], b.turns_of(2, 48))
                            if n >= 2 or b.has(1):
                                pe.wait_ge(exp_done, b.count(UNITS, n - 1))
                            S, Q, K = sexp[n % 2], qs[b.four], kd[b.four]
                            if kind < 2:
                                hp = 2 * g + kind
                                last = mm(S[:, :], K[0:STACK + MROWS, hp, 0:128],
                                          Q[0:STACK + MROWS, hp, :, :].rearrange("p s t -> p (s t)"), True, True)
                            else:
                                for j in range(2):
                                    hp = 2 * g + j
                                    last = mm(S[:, 256 * j:256 * j + 256], K[0:STACK + MROWS, hp, 128:256],
                                              Q[0:STACK + MROWS, hp, :, 128:256], True, True)
                            last.then_inc(sexp_ps, 1)
                    for n in range(UNITS):
                        b = st.batch(slot, T_MAX + n)
                        if b:
                            g, kind = n // 3, n % 3
                            if n == 0:
                                pe.wait_ge(stacked[b.four], b.turns_of(4, 16 * 12))
                            if n >= 2 or b.has(1):
                                pe.wait_ge(max_done, b.count(UNITS, n - 1))
                            S, Q, K = smax[n % 2], qs[b.four], kd[b.four]
                            if kind == 0:
                                causal_mask(S[:, :], 4)
                                for j in range(4):
                                    hp, ab = 2 * g + j // 2, j % 2
                                    last = mm(S[:, 128 * j:128 * j + 128], Q[0:STACK, hp, ab, 0:128],
                                              K[0:STACK, hp, 0:128], False, True)
                            else:
                                hp = 2 * g + kind - 1
                                causal_mask(S[:, :].rearrange("p (h t) -> p h t", h=2)[:, :, 128:256], 2)
                                for ab in range(2):
                                    last = mm(S[:, 256 * ab:256 * ab + 256], Q[0:STACK, hp, ab, 128:256],
                                              K[0:STACK, hp, :], False, True)
                            last.then_inc(smax_ps, 1)
                    for g in range(4):
                        b = st.batch(slot, T_PV + 3 * g)
                        if b:
                            pe.wait_ge(causal_done, b.count(8, 2 * g + 2))
                            if g == 0:
                                pe.wait_ge(v_ready, b.count(1, 1))
                            if g % 2 == 0 and b.has(1):
                                pe.wait_ge(oraw_ready, b.count(2, g // 2 - 1))
                            P, V, c = probs[b.two], vaug[b.four], 256 * (g % 2)
                            O = pvps[g // 2]
                            for q in range(4):
                                mm(O[32 * q:32 * q + 32, c:c + 256], V[:, 0, 4 * g + q, :],
                                   P[:, 3 * g + q // 2, 256 * (q % 2):256 * (q % 2) + 256], True, False)
                            for q in range(4):
                                last = mm(O[32 * q:32 * q + 32, c + 128:c + 256], V[:, 1, 4 * g + q, :],
                                          P[:, 3 * g + 2, 128 * q:128 * q + 128], False, True)
                            last.then_inc(pv_ps, 1)


_INS = ['L0_attn_x', 'L0_attn_w_qkv', 'L0_attn_w_o', 'L0_ffn_Wq', 'L0_ffn_routers', 'L0_ffn_leaf_keys',
        'L0_ffn_leaf_values', 'L0_ffn_Wout_w', 'L0_ffn_Wout_b']
_OUTS = [((BATCHES, SEQ, D), 'float32')]


def kernel(**inputs):
    import numpy as _np
    import concourse.bacc as _bacc
    from concourse import mybir as _mybir
    from concourse.bass_utils import run_bass_kernel_spmd as _run

    nc = _bacc.Bacc("TRN2", target_bir_lowering=False, num_devices=1)
    arrays, args = {}, []
    for name in _INS:
        a = _np.ascontiguousarray(inputs[name])
        arrays[f"in_{name}_dram"] = a
        args.append(nc.dram_tensor(f"in_{name}_dram", a.shape, _mybir.dt.from_np(a.dtype), kind="ExternalInput").ap())
    for i, (shape, dtype) in enumerate(_OUTS):
        dt = _mybir.dt.from_np(_np.dtype(dtype))
        args.append(nc.dram_tensor(f"out_{i}_dram", shape, dt, kind="ExternalOutput").ap())
    sandwich_kernel(nc, *args)
    r = _run(nc, [arrays], core_ids=[0])
    got = tuple(r.results[0][f"out_{i}_dram"] for i in range(len(_OUTS)))
    return got[0]
```

```python
from contextlib import ExitStack

import numpy as np

import concourse.bass as bass
from concourse import mybir

ALU = mybir.AluOpType
ACT = mybir.ActivationFunctionType
AX_X = mybir.AxisListType.X
F32 = mybir.dt.float32
BF16 = mybir.dt.bfloat16

BATCHES, SEQ, D = 32, 256, 128
HEADS, DK = 16, 8
TILE = 128
PAIRS = HEADS // 2
LEVELS = 8
NODES = 2**LEVELS - 1
GATES = NODES + 1
HALF = 2 ** (LEVELS - 1)
EPS = 1e-5
MASKED = -3.0e38
PARTS = ((0, 0), (1, 0), (2, 0), (0, 1), (1, 1), (0, 2))
STACK = len(PARTS) * 2 * DK
MROWS = 3
BANK = 512
UNITS = 12
MASKED_BY_PE = (0, 2)
SLOTS = 12
TURN = 8

T_LOAD = 0
T_LN1_STATS, T_LN1_NORM = 4, 7
J_XT = 9
J_QK, T_QK_REST, T_QK_LOW, T_STACK = 11, 12, 15, 16
J_V = 27
T_MAX = 24
J_M, T_MREST, T_MLOW, T_MROWS = 37, 38, 38, 39
T_EXP = 42
T_CAUSAL0, T_CAUSAL1 = 45, 45
T_PV = (50, 55, 56, 57)
T_ORAW = 58
T_RELOAD = 55
J_O = 62
J_OT, J_Y = 64, 66
T_LN2_STATS, T_LN2_NORM, T_X1 = 66, 68, 67
T_LN3_STATS = 69
J_X1T, J_Z = 70, 77
T_TREE = 77
J_LPT, J_RET = 84, 92
T_LN4_STATS, T_LN4_NORM, T_OUT, T_STORE = 92, 94, 94, 96
MISC_JOBS = (J_XT, J_QK, J_V, J_M, J_O, J_OT, J_Y, J_X1T, J_Z, J_LPT, J_RET)
LAST = T_STORE // SLOTS
ITERATIONS = BATCHES + LAST
LOOP_FROM, LOOP_TO = 8, 32
assert LOOP_FROM >= LAST and LOOP_TO <= BATCHES and LOOP_FROM % TURN == 0 and LOOP_TO % TURN == 0
assert len({t % SLOTS for t in MISC_JOBS}) == len(MISC_JOBS)


class Batch:

    def __init__(self, turn, at):
        self.turn, self.at = turn, at
        self.least = (turn if isinstance(turn, int) else LOOP_FROM // TURN) * TURN + at
        self.index = turn * TURN + at
        self.live = 0 <= self.least < BATCHES
        self.two, self.four = at % 2, at % 4

    def has(self, back):
        return self.least >= back

    def count(self, per, plus):
        return self.turn * (TURN * per) + (self.at * per + plus)

    def turns_of(self, ring, per, back=0):
        return self.turn * (TURN // ring * per) + ((self.at - back) // ring + 1) * per


class Step:

    def __init__(self, turn, at):
        self.turn, self.at = turn, at
        self.number = turn * TURN + at if isinstance(turn, int) else None

    def batch(self, slot, time):
        if (time - slot) % SLOTS:
            return None
        b = Batch(self.turn, self.at - (time - slot) // SLOTS)
        return b if b.live else None


def steps(eng):
    for i in range(LOOP_FROM):
        yield Step(i // TURN, i % TURN)
    with eng.Fori(LOOP_FROM // TURN, LOOP_TO // TURN) as turn:
        for u in range(TURN):
            yield Step(turn, u)
    for i in range(LOOP_TO, ITERATIONS):
        yield Step(i // TURN, i % TURN)


def sandwich_kernel(nc, x, w_qkv, w_o, Wq, routers, leaf_keys, leaf_values, Wout_w, Wout_b, out):
    x_v = x.rearrange("b (t p) d -> b p t d", p=TILE)
    out_v = out.rearrange("b (t p) d -> b p t d", p=TILE)

    with ExitStack() as ctx:
        def sb(name, shape, dt=F32):
            return ctx.enter_context(nc.sbuf_tensor(name, shape, dt))

        def sem(name):
            return ctx.enter_context(nc.semaphore(name))

        misc = [ctx.enter_context(nc.psum_tensor(f"misc{i}", [128, BANK], F32)) for i in range(2)]
        smax = [ctx.enter_context(nc.psum_tensor(f"smax{i}", [128, BANK], F32)) for i in range(3)]
        sexp = [ctx.enter_context(nc.psum_tensor(f"sexp{i}", [128, BANK], F32)) for i in range(2)]
        pvps = ctx.enter_context(nc.psum_tensor("pvps", [128, BANK], F32))

        ident = sb("ident", [128, 128])
        identb = sb("identb", [128, 128], BF16)
        mask = sb("mask", [128, 128], BF16)
        mask2 = sb("mask2", [128, 2, 128])
        masked1 = sb("masked1", [128, 4, 128], BF16)
        masked2 = sb("masked2", [128, 2, 2, 256], BF16)
        ones1 = sb("ones1", [1, 128])
        neghalf = sb("neghalf", [128, 2])
        eps = sb("eps", [128, 2])
        zero2 = sb("zero2", [128, 2])
        wraw = sb("wraw", [128, 9, 128])
        wT = sb("wT", [128, 9, 128])
        rraw = sb("rraw", [127, 128])
        rT = sb("rT", [128, GATES])
        wqk = sb("wqk", [128, 2, 128])
        wg = sb("wg", [128, GATES])
        lva = sb("lva", [128, 128])
        lvb = sb("lvb", [128, 128])
        lvd = sb("lvd", [128, 3, 128])
        woc = sb("woc", [128, 128])
        cstats = sb("cstats", [128, 4, 6])
        cmean = sb("cmean", [128, 4, 2])
        bias0 = sb("bias0", [1, 128])
        wqc = sb("wqc", [128, 128])

        xin = [sb(f"xin{i}", [128, 2, 128]) for i in range(2)]
        xn = [sb(f"xn{i}", [128, 2, 128]) for i in range(2)]
        xT = [sb(f"xT{i}", [128, 256]) for i in range(2)]
        parts = [sb(f"parts{i}", [128, 6, 256], BF16) for i in range(2)]
        rest = [sb(f"rest{i}", [128, 2, 256]) for i in range(2)]
        qsec = [sb(f"qsec{i}", [128, 2, 3, 256], BF16) for i in range(2)]
        qs = [sb(f"qs{i}", [128, PAIRS, 2, 256], BF16) for i in range(4)]
        kd = [sb(f"kd{i}", [128, PAIRS, 256], BF16) for i in range(4)]
        vaug = [sb(f"vaug{i}", [128, 2, PAIRS, 2, 32]) for i in range(4)]
        mx = [sb(f"mx{i}", [128, HEADS, 2]) for i in range(2)]
        mrest = [sb(f"mrest{i}", [32, 128]) for i in range(2)]
        mparts = [sb(f"mparts{i}", [32, 3, 128], BF16) for i in range(2)]
        probs = [sb(f"probs{i}", [128, UNITS, BANK]) for i in range(2)]
        oraw = [sb(f"oraw{i}", [128, BANK]) for i in range(2)]
        onorm = [sb(f"onorm{i}", [128, 2, HEADS, DK]) for i in range(2)]
        rden = [sb(f"rden{i}", [128, 2 * HEADS, 1]) for i in range(2)]
        oT = [sb(f"oT{i}", [128, 256]) for i in range(2)]
        y = [sb(f"y{i}", [128, 2, 128]) for i in range(2)]
        yn = [sb(f"yn{i}", [128, 2, 128]) for i in range(2)]
        xres = [sb(f"xres{i}", [128, 2, 128]) for i in range(2)]
        x1 = [sb(f"x1{i}", [128, 2, 128]) for i in range(4)]
        x1T = [sb(f"x1T{i}", [128, 256]) for i in range(2)]
        u = [sb(f"u{i}", [128, 2, GATES]) for i in range(2)]
        tree = [sb(f"tree{i}", [128, 2, 256]) for i in range(2)]
        right = [sb(f"right{i}", [128, 2, HALF]) for i in range(2)]
        lpT = [sb(f"lpT{i}", [128, 2, 2, 128]) for i in range(2)]
        ret = [sb(f"ret{i}", [128, 2, 128]) for i in range(2)]
        retn = [sb(f"retn{i}", [128, 2, 128]) for i in range(2)]
        outb = [sb(f"outb{i}", [128, 2, 128]) for i in range(2)]
        stats = [[sb(f"stats{k}_{i}", [128, 2, 6]) for i in range(2)] if k in (0, 2) else None for k in range(4)]
        mv = [[sb(f"mv{k}_{i}", [128, 2, 2]) for i in range(2)] if k in (0, 2) else None for k in range(4)]
        vare = [[sb(f"vare{k}_{i}", [128, 2]) for i in range(2)] for k in range(4)]
        rstd = [[sb(f"rstd{k}_{i}", [128, 2]) for i in range(2)] for k in range(4)]
        msq = [[sb(f"msq{k}_{i}", [128, 2]) for i in range(2)] if k in (1, 3) else None for k in range(4)]
        square = sb("square", [128, 2, 2, 2, 128])
        mr = [sb(f"mr{i}", [128, 2]) for i in range(2)]
        nmr = [sb(f"nmr{i}", [128, 2]) for i in range(2)]

        w_loaded = sem("w_loaded")
        bias_loaded = sem("bias_loaded")
        zeroed = sem("zeroed")
        const_ready = sem("const_ready")
        vset = sem("vset")
        w_turned = sem("w_turned")
        w_copied = sem("w_copied")
        w_fused = sem("w_fused")
        lv_step = sem("lv_step")
        centre_step = sem("centre_step")
        w_ready = sem("w_ready")
        buffers_set = sem("buffers_set")
        kd_set = sem("kd_set")

        x_loaded = [sem(f"x_loaded{i}") for i in range(2)]
        xres_loaded = [sem(f"xres_loaded{i}") for i in range(2)]
        stacked = [sem(f"stacked{i}") for i in range(4)]
        mrows_in = [sem(f"mrows_in{i}") for i in range(2)]
        stored = [sem(f"stored{i}") for i in range(2)]
        stats_done = [sem(f"stats_done{k}") for k in range(4)]
        mv_ready = [sem(f"mv_ready{k}") for k in range(4)]
        rstd_step = [sem(f"rstd_step{k}") for k in range(4)]
        xn_ready = sem("xn_ready")
        xT_ps = sem("xT_ps")
        xT_ready = sem("xT_ready")
        qk_ps = sem("qk_ps")
        v_ps = sem("v_ps")
        hi_ready = sem("hi_ready")
        rest_ready = sem("rest_ready")
        mid_ready = sem("mid_ready")
        lo_ready = sem("lo_ready")
        qsec_ready = sem("qsec_ready")
        v_ready = sem("v_ready")
        smax_ps = sem("smax_ps")
        max_done = sem("max_done")
        m_ps = sem("m_ps")
        m_step = sem("m_step")
        sexp_ps = sem("sexp_ps")
        exp_done = sem("exp_done")
        causal_done = sem("causal_done")
        pv_ps = sem("pv_ps")
        oraw_ready = sem("oraw_ready")
        o_ps = sem("o_ps")
        rden_ready = sem("rden_ready")
        onorm_ready = sem("onorm_ready")
        oT_ps = sem("oT_ps")
        oT_ready = sem("oT_ready")
        y_ps = sem("y_ps")
        y_ready = sem("y_ready")
        yn_ready = sem("yn_ready")
        x1_ready = sem("x1_ready")
        x1T_ps = sem("x1T_ps")
        x1T_ready = sem("x1T_ready")
        z_ps = sem("z_ps")
        u_ready = sem("u_ready")
        tree_step = sem("tree_step")
        lpT_ps = sem("lpT_ps")
        lpT_ready = sem("lpT_ready")
        ret_ps = sem("ret_ps")
        ret_ready = sem("ret_ready")
        retn_ready = sem("retn_ready")
        out_ready = sem("out_ready")
        TREE = 2 * (LEVELS - 1) + 1

        w_src = [w_qkv[i].rearrange("h k m -> (h k) m") for i in range(3)] + [
            w_o, Wout_w, Wq, routers[0:128, :], leaf_values[0:128, :], leaf_values[128:256, :]]
        W_Q, W_K, W_V, W_O, W_OUT, W_FQ, W_R0, W_L0, W_L1 = range(9)

        block = ctx.enter_context(nc.Block())

        @block.sync
        def _(sp):
            for st in steps(sp):
                for slot in range(SLOTS):
                    b = st.batch(slot, T_LOAD)
                    if b:
                        if b.has(2):
                            sp.wait_ge(xn_ready, b.count(2, -2))
                        sp.dma_start(xin[b.two][:, :, :], x_v[b.index]).then_inc(x_loaded[b.two], 16)
                    if st.number == 0 and slot == T_LOAD:
                        for j, src in enumerate(w_src):
                            sp.dma_start(wraw[:, j, :], src).then_inc(w_loaded, 16)
                        sp.dma_start(rraw[:, :], routers[128:NODES, :]).then_inc(w_loaded, 16)
                        sp.dma_start(bias0[:, :], Wout_b.rearrange("(a d) -> a d", a=1)).then_inc(bias_loaded, 16)
                    b = st.batch(slot, T_STACK)
                    if b:
                        if b.has(4):
                            sp.wait_ge(sexp_ps, b.count(UNITS, -3 * UNITS))
                        for j, (_, part) in enumerate(PARTS):
                            if part == 0:
                                sp.wait_ge(hi_ready, b.count(1, 1))
                            elif part == 1:
                                sp.wait_ge(mid_ready, b.count(1, 1))
                            else:
                                sp.wait_ge(lo_ready, b.count(1, 1))
                            sp.dma_start(kd[b.four][16 * j:16 * j + 16, :, :],
                                         parts[b.two][:, 5 - part, :]).then_inc(stacked[b.four], 16)
                        sp.wait_ge(qsec_ready, b.count(2, 2))
                        for j, (part, _) in enumerate(PARTS):
                            sp.dma_start(qs[b.four][16 * j:16 * j + 16, :, :, :].rearrange("p h s t -> p h (s t)"),
                                         qsec[b.two][:, :, part, :]
                                         ).then_inc(stacked[b.four], 16)
                    b = st.batch(slot, T_MROWS)
                    if b:
                        sp.wait_ge(m_step, b.count(4, 4))
                        for j in range(MROWS):
                            sp.dma_start(qs[b.four][STACK + j:STACK + j + 1, :, :, :].rearrange("p h s t -> p (h s t)"),
                                         mparts[b.two][:, j, :]).then_inc(mrows_in[b.two], 16)
                    b = st.batch(slot, T_RELOAD)
                    if b:
                        if b.has(2):
                            sp.wait_ge(x1_ready, b.count(1, -1))
                        sp.dma_start(xres[b.two][:, :, :], x_v[b.index]).then_inc(xres_loaded[b.two], 16)
                    b = st.batch(slot, T_STORE)
                    if b:
                        sp.wait_ge(out_ready, b.count(1, 1))
                        sp.dma_start(out_v[b.index], outb[b.two][:, :, :]).then_inc(stored[b.two], 16)
            for i in range(2):
                sp.wait_ge(stored[i], 16 * (BATCHES // 2))

        @block.gpsimd
        def _(pool):
            nc.gpsimd.memset(ident[:, :], 0.0).then_inc(zeroed, 1)
            nc.gpsimd.memset(identb[:, :], 0.0).then_inc(zeroed, 1)
            nc.gpsimd.memset(mask[:, :], 0.0).then_inc(zeroed, 1)
            nc.gpsimd.memset(ones1[:, :], 1.0).then_inc(const_ready, 1)
            nc.gpsimd.memset(mask2[:, :, :], 0.0).then_inc(zeroed, 1)
            nc.gpsimd.memset(neghalf[:, :], -0.5).then_inc(const_ready, 1)
            nc.gpsimd.memset(eps[:, :], EPS).then_inc(zeroed, 1)
            nc.gpsimd.memset(zero2[:, :], 0.0).then_inc(const_ready, 1)
            pool.wait_ge(zeroed, 5)
            nc.gpsimd.affine_select(out=ident[:, :], in_=ident[:, :], compare_op=ALU.not_equal, fill=1.0,
                                    base=0, pattern=[[-1, 128]], channel_multiplier=1).then_inc(const_ready, 1)
            nc.gpsimd.affine_select(out=identb[:, :], in_=identb[:, :], compare_op=ALU.not_equal, fill=1.0,
                                    base=0, pattern=[[-1, 128]], channel_multiplier=1).then_inc(const_ready, 1)
            nc.gpsimd.affine_select(out=mask[:, :], in_=mask[:, :], compare_op=ALU.is_ge, fill=MASKED,
                                    base=0, pattern=[[-1, 128]], channel_multiplier=1).then_inc(const_ready, 1)
            nc.gpsimd.affine_select(out=mask2[:, 1, :], in_=mask2[:, 1, :], compare_op=ALU.is_ge, fill=MASKED,
                                    base=0, pattern=[[-1, 128]], channel_multiplier=1).then_inc(const_ready, 1)
            def rstd_of(k, b):
                two, step = b.two, rstd_step[k]
                steps_each = 4 if k == 0 else 2
                pool.wait_ge(mv_ready[k], b.count(2, 2))
                if k == 2 and b.has(2):
                    pool.wait_ge(u_ready, b.count(1, -1))
                variance = msq[k][two][:, :] if k in (1, 3) else mv[k][two][:, :, 1]
                nc.gpsimd.tensor_tensor(vare[k][two][:, :], variance, eps[:, :],
                                        ALU.add).then_inc(step, 1)
                pool.wait_ge(step, b.count(steps_each, 1))
                nc.gpsimd.tensor_tensor(rstd[k][two][:, :], vare[k][two][:, :], neghalf[:, :],
                                        ALU.pow).then_inc(step, 1)
                if k == 0:
                    pool.wait_ge(step, b.count(4, 2))
                    nc.gpsimd.tensor_tensor(mr[two][:, :], mv[k][two][:, :, 0], rstd[k][two][:, :],
                                            ALU.mult).then_inc(step, 1)
                    pool.wait_ge(step, b.count(4, 3))
                    nc.gpsimd.tensor_tensor(nmr[two][:, :], zero2[:, :], mr[two][:, :],
                                            ALU.subtract).then_inc(step, 1)

            def causal(b, units, view):
                pool.wait_ge(exp_done, b.count(UNITS, units))
                pool.nop(nofuse=True)
                nc.gpsimd.affine_select(out=view, in_=view, compare_op=ALU.is_ge, fill=0.0, base=0,
                                        pattern=[[0, 4], [1, 128]], channel_multiplier=-1
                                        ).then_inc(causal_done, 1)

            for st in steps(pool):
                for slot in range(SLOTS):
                    b = st.batch(slot, T_LN1_STATS)
                    if b:
                        rstd_of(0, b)
                    b = st.batch(slot, T_QK_LOW)
                    if b:
                        pool.wait_ge(mid_ready, b.count(1, 1))
                        nc.gpsimd.tensor_tensor(parts[b.two][:, 2:4, :], rest[b.two][:, :, :],
                                                parts[b.two][:, 1:5:3, :], ALU.subtract).then_inc(lo_ready, 1)
                    for g in range(4):
                        b = st.batch(slot, T_CAUSAL0 + 3 * g)
                        if b:
                            causal(b, 3 * g + 2, probs[b.two][:, 3 * g:3 * g + 2, :].rearrange(
                                "p u (h s) -> p (u h) s", h=2)[:, :, 0:128])
                        b = st.batch(slot, T_CAUSAL1 + 3 * g)
                        if b:
                            causal(b, 3 * g + 3, probs[b.two][:, 3 * g + 2, :].rearrange(
                                "p (h s) -> p h s", h=4))
                    b = st.batch(slot, T_MLOW)
                    if b:
                        pool.wait_ge(m_step, b.count(4, 3))
                        nc.gpsimd.tensor_tensor(mparts[b.two][:, 2, :], mrest[b.two][:, :], mparts[b.two][:, 1, :],
                                                ALU.subtract).then_inc(m_step, 1)
                    b = st.batch(slot, T_LN2_STATS)
                    if b:
                        rstd_of(1, b)
                    b = st.batch(slot, T_X1)
                    if b:
                        pool.wait_ge(yn_ready, b.count(2, 2))
                        pool.wait_ge(xres_loaded[b.two], b.turns_of(2, 16))
                        nc.gpsimd.tensor_tensor(x1[b.four][:, :, :], xres[b.two][:, :, :], yn[b.two][:, :, :],
                                                ALU.add).then_inc(x1_ready, 1)
                    b = st.batch(slot, T_LN3_STATS)
                    if b:
                        rstd_of(2, b)
                    b = st.batch(slot, T_LN4_STATS)
                    if b:
                        rstd_of(3, b)
                    b = st.batch(slot, T_OUT)
                    if b:
                        pool.wait_ge(retn_ready, b.count(2, 2))
                        if b.has(2):
                            pool.wait_ge(stored[b.two], b.turns_of(2, 16, 2))
                        nc.gpsimd.tensor_tensor(outb[b.two][:, :, :], x1[b.four][:, :, :], retn[b.two][:, :, :],
                                                ALU.add).then_inc(out_ready, 1)

        @block.scalar
        def _(act):
            def copy(dst, src):
                return nc.scalar.activation(dst, src, ACT.Copy)

            def halve(dst, src):
                return nc.scalar.activation(dst, src, ACT.Copy, scale=0.5)

            act.wait_ge(w_turned, 1)
            copy(wT[:, W_V, :], misc[0][:, 256:384]).then_inc(w_copied, 1)
            for j in (W_Q, W_K):
                copy(wqk[:, j, :].rearrange("p (a d h) -> p a d h", a=2, d=DK),
                     misc[0][:, 128 * j:128 * j + 128].rearrange("p (h a d) -> p a d h", a=2, d=DK)
                     ).then_inc(w_copied, 1)
            copy(wT[:, W_O, :], misc[0][:, 384:512]).then_inc(w_copied, 1)
            act.wait_ge(w_turned, 2)
            halve(rT[:, 0:128], misc[1][:, 0:128]).then_inc(w_copied, 1)
            copy(wT[:, W_L0:W_L1 + 1, :].rearrange("p a n -> p (a n)"), misc[1][:, 128:384]).then_inc(w_copied, 1)
            copy(wT[:, W_OUT, :], misc[1][:, 384:512]).then_inc(w_copied, 1)
            act.wait_ge(w_turned, 3)
            halve(rT[:, 128:NODES], smax[0][:, 0:127]).then_inc(w_copied, 1)
            act.wait_ge(w_fused, 1)
            copy(wg[:, 0:NODES], smax[1][:, 0:NODES]).then_inc(w_ready, 1)

            def mean_squares(k, b, src):
                for t in range(2):
                    nc.scalar.activation(square[:, k // 2, b.two, t, :], src[:, 128 * t:128 * t + 128], ACT.Square,
                                         scale=float(D) ** -0.5, accum_out=msq[k][b.two][:, t:t + 1]
                                         ).then_inc(mv_ready[k], 1)

            def scale_rows(k, b, dst, src, ready):
                for t in range(2):
                    nc.scalar.activation(dst[:, t, :], src[:, t, :], ACT.Copy, scale=rstd[k][b.two][:, t:t + 1]
                                         ).then_inc(ready, 1)

            for st in steps(act):
                for slot in range(SLOTS):
                    b = st.batch(slot, T_LN1_NORM)
                    if b:
                        act.wait_ge(rstd_step[0], b.count(4, 4))
                        if b.has(2):
                            act.wait_ge(xT_ps, b.count(1, -1))
                        for t in range(2):
                            nc.scalar.activation(xn[b.two][:, t, :], xin[b.two][:, t, :], ACT.Identity,
                                                 bias=nmr[b.two][:, t:t + 1], scale=rstd[0][b.two][:, t:t + 1]
                                                 ).then_inc(xn_ready, 1)
                    b = st.batch(slot, J_XT)
                    if b:
                        act.wait_ge(xT_ps, b.count(1, 1))
                        if b.has(2):
                            act.wait_ge(qk_ps, b.count(1, -1))
                            act.wait_ge(v_ps, b.count(1, -1))
                        copy(xT[b.two][:, :], misc[slot % 2][:, 0:256]).then_inc(xT_ready, 1)
                    b = st.batch(slot, J_QK)
                    if b:
                        act.wait_ge(qk_ps, b.count(1, 1))
                        if b.has(2):
                            act.wait_ge(stacked[(b.four + 2) % 4], b.turns_of(4, 16 * 12, 2))
                        copy(parts[b.two][:, 0::5, :], misc[slot % 2][:, :].rearrange("p (a n) -> p a n", a=2)
                             ).then_inc(hi_ready, 1)
                    b = st.batch(slot, T_QK_LOW)
                    if b:
                        act.wait_ge(rest_ready, b.count(1, 1))
                        copy(parts[b.two][:, 1:5:3, :], rest[b.two][:, :, :]).then_inc(mid_ready, 1)
                    b = st.batch(slot, J_V)
                    if b:
                        act.wait_ge(v_ps, b.count(1, 1))
                        if b.has(4):
                            act.wait_ge(pv_ps, b.count(4, -12))
                        else:
                            act.wait_ge(buffers_set, 1)
                        for ab in range(2):
                            last = copy(vaug[b.four][:, :, :, ab, 16 * ab:16 * ab + DK],
                                        misc[slot % 2][:, 0:256].rearrange("p (t h a d) -> p a t h d", t=2, a=2, d=DK)[:, ab])
                        last.then_inc(v_ready, 1)
                    b = st.batch(slot, T_ORAW)
                    if b:
                        act.wait_ge(pv_ps, b.count(4, 4))
                        if b.has(2):
                            act.wait_ge(o_ps, b.count(1, -1))
                        copy(oraw[b.two][:, :], pvps[:, :]).then_inc(oraw_ready, 1)
                    b = st.batch(slot, J_OT)
                    if b:
                        act.wait_ge(oT_ps, b.count(1, 1))
                        if b.has(2):
                            act.wait_ge(y_ps, b.count(1, -1))
                        copy(oT[b.two][:, :], misc[slot % 2][:, 0:256]).then_inc(oT_ready, 1)
                    b = st.batch(slot, J_Y)
                    if b:
                        act.wait_ge(y_ps, b.count(1, 1))
                        mean_squares(1, b, misc[slot % 2])
                        copy(y[b.two][:, :, :].rearrange("p t n -> p (t n)"), misc[slot % 2][:, 0:256]
                             ).then_inc(y_ready, 1)
                    b = st.batch(slot, T_LN2_NORM)
                    if b:
                        act.wait_ge(rstd_step[1], b.count(2, 2))
                        if b.has(2):
                            act.wait_ge(x1_ready, b.count(1, -1))
                        act.wait_ge(y_ready, b.count(1, 1))
                        scale_rows(1, b, yn[b.two], y[b.two], yn_ready)
                    b = st.batch(slot, J_X1T)
                    if b:
                        act.wait_ge(x1T_ps, b.count(1, 1))
                        if b.has(2):
                            act.wait_ge(z_ps, b.count(1, -1))
                        copy(x1T[b.two][:, :], misc[slot % 2][:, 0:256]).then_inc(x1T_ready, 1)
                    b = st.batch(slot, J_Z)
                    if b:
                        act.wait_ge(z_ps, b.count(1, 1))
                        act.wait_ge(rstd_step[2], b.count(2, 2))
                        if b.has(2):
                            act.wait_ge(tree_step, b.count(TREE, -TREE))
                        for t in range(2):
                            last = nc.scalar.activation(u[b.two][:, t, :], misc[slot % 2][:, GATES * t:GATES * t + GATES],
                                                        ACT.Tanh, scale=rstd[2][b.two][:, t:t + 1])
                        last.then_inc(u_ready, 1)
                    b = st.batch(slot, J_LPT)
                    if b:
                        act.wait_ge(lpT_ps, b.count(1, 1))
                        if b.has(2):
                            act.wait_ge(ret_ps, b.count(1, -1))
                        copy(lpT[b.two][:, :, :, :].rearrange("p t a n -> p (t a n)"), misc[slot % 2][:, :]
                             ).then_inc(lpT_ready, 1)
                    b = st.batch(slot, J_RET)
                    if b:
                        act.wait_ge(ret_ps, b.count(1, 1))
                        mean_squares(3, b, misc[slot % 2])
                        copy(ret[b.two][:, :, :].rearrange("p t n -> p (t n)"), misc[slot % 2][:, 0:256]
                             ).then_inc(ret_ready, 1)
                    b = st.batch(slot, T_LN4_NORM)
                    if b:
                        act.wait_ge(rstd_step[3], b.count(2, 2))
                        if b.has(2):
                            act.wait_ge(out_ready, b.count(1, -1))
                        act.wait_ge(ret_ready, b.count(1, 1))
                        scale_rows(3, b, retn[b.two], ret[b.two], retn_ready)
                    for n in range(UNITS):
                        b = st.batch(slot, T_EXP + n)
                        if b:
                            act.wait_ge(sexp_ps, b.count(UNITS, n + 1))
                            if b.has(2):
                                act.wait_ge(pv_ps, b.count(4, -8 + 2 * (n // 6) + 2))
                            nc.scalar.activation(probs[b.two][:, n, :], sexp[n % 2][:, :], ACT.Exp,
                                                 scale=float(DK) ** -0.5).then_inc(exp_done, 1)

        @block.vector
        def _(dve):
            for i in range(2):
                nc.vector.memset(qsec[i][:, :, :, :], 0.0).then_inc(vset, 1)
            nc.vector.memset(wg[:, NODES:GATES], 0.0).then_inc(vset, 1)
            for i in range(4):
                nc.vector.memset(vaug[i][:, :, :, :, :], 0.0).then_inc(vset, 1)
            dve.wait_ge(vset, 7)
            dve.wait_ge(const_ready, 7)
            for i in range(4):
                for ab in range(2):
                    last = nc.vector.memset(vaug[i][:, :, :, ab, 16 * ab + DK:16 * ab + DK + 1], 1.0)
            last.then_inc(buffers_set, 1)
            centred = [0]

            def centre(dst, src, rows):
                n = centred[0]
                centred[0] += 1
                nc.vector.bn_stats(cstats[0:rows, n, :], src).then_inc(centre_step, 1)
                dve.wait_ge(centre_step, 3 * n + 1)
                nc.vector.bn_aggr(cmean[0:rows, n, :], cstats[0:rows, n, :]).then_inc(centre_step, 1)
                dve.wait_ge(centre_step, 3 * n + 2)
                nc.vector.tensor_scalar(dst, src, cmean[0:rows, n, 0:1], None, ALU.subtract).then_inc(centre_step, 1)
                dve.wait_ge(centre_step, 3 * n + 3)

            dve.wait_ge(w_loaded, 160)
            centre(wqc[:, :], wraw[:, W_FQ, :], 128)

            def centre_weights():
                dve.wait_ge(w_copied, 4)
                centre(woc[:, :], wT[:, W_O, :], 128)
                dve.wait_ge(w_fused, 2)
                nc.vector.tensor_scalar(lvd[:, 0, :], sexp[0][:, 0:128], 0.5 ** (LEVELS - 1), None, ALU.mult).then_inc(lv_step, 1)
                nc.vector.tensor_scalar(lvd[:, 1, :], sexp[0][:, 128:256], 0.5 ** LEVELS, None, ALU.mult).then_inc(lv_step, 1)
                dve.wait_ge(lv_step, 2)
                centre(lva[:, :], lvd[:, 0, :], 128)
                centre(lvd[:, 2, :], lvd[:, 1, :], 128)
                nc.vector.scalar_tensor_tensor(out=lvb[:, :], in0=lva[:, :], scalar=-0.5, in1=lvd[:, 2, :],
                                               op0=ALU.mult, op1=ALU.add).then_inc(w_ready, 1)

            def stats_of(k, b, src):
                for t in range(2):
                    nc.vector.bn_stats(stats[k][b.two][:, t, :], src[:, t, :]).then_inc(stats_done[k], 1)

            def aggregate(k, b):
                for t in range(2):
                    dve.wait_ge(stats_done[k], b.count(2, t + 1))
                    dve.nop(nofuse=True)
                    nc.vector.bn_aggr(mv[k][b.two][:, t, :], stats[k][b.two][:, t, :]).then_inc(mv_ready[k], 1)

            def tree_level(b, k):
                U, L, n = u[b.two], tree[b.two], 2**k
                if k == 0:
                    dve.wait_ge(u_ready, b.count(1, 1))
                    if b.has(2):
                        dve.wait_ge(lpT_ps, b.count(1, -1))
                    nc.vector.tensor_scalar(L[:, :, 2:3], U[:, :, 0:1], -1.0, 1.0, ALU.mult, ALU.add
                                            ).then_inc(tree_step, 1)
                    nc.vector.tensor_scalar(L[:, :, 3:4], U[:, :, 0:1], 1.0, None, ALU.add).then_inc(tree_step, 1)
                    return
                dve.wait_ge(tree_step, b.count(TREE, 2 * k))
                if k < LEVELS - 1:
                    nc.vector.scalar_tensor_tensor(
                        out=L[:, :, 2 * n:4 * n:2], in0=U[:, :, n - 1:2 * n - 1], scalar=1.0,
                        in1=L[:, :, n:2 * n], op0=ALU.subtract, op1=ALU.mult, reverse0=True).then_inc(tree_step, 1)
                dst = L[:, :, 2 * n + 1:4 * n:2] if k < LEVELS - 1 else right[b.two][:, :, :]
                nc.vector.scalar_tensor_tensor(
                    out=dst, in0=U[:, :, n - 1:2 * n - 1], scalar=1.0,
                    in1=L[:, :, n:2 * n], op0=ALU.add, op1=ALU.mult).then_inc(tree_step, 1)

            for st in steps(dve):
                for slot in range(SLOTS):
                    if st.number in (1, 2) and slot == 0:
                        for i in range(2 * st.number - 2, 2 * st.number):
                            nc.vector.memset(kd[i][96:128, :, :], -1.0).then_inc(kd_set, 1)
                    if st.number == 2 and slot == 0:
                        centre_weights()
                    b = st.batch(slot, T_LN1_STATS)
                    if b:
                        dve.wait_ge(x_loaded[b.two], b.turns_of(2, 16))
                        stats_of(0, b, xin[b.two])
                    b = st.batch(slot, T_QK_REST)
                    if b:
                        dve.wait_ge(hi_ready, b.count(1, 1))
                        if b.has(2):
                            dve.wait_ge(lo_ready, b.count(1, -1))
                        nc.vector.tensor_tensor(rest[b.two][:, :, :],
                                                misc[J_QK % 2][:, :].rearrange("p (a n) -> p a n", a=2),
                                                parts[b.two][:, 0::5, :], ALU.subtract).then_inc(rest_ready, 1)
                    b = st.batch(slot, J_M)
                    if b:
                        dve.wait_ge(m_ps, b.count(1, 1))
                        if b.has(2):
                            dve.wait_ge(mrows_in[b.two], b.turns_of(2, 48, 2))
                        nc.vector.tensor_copy(mparts[b.two][:, 0, :], misc[J_M % 2][0:32, 0:128]).then_inc(m_step, 1)
                    b = st.batch(slot, T_MREST)
                    if b:
                        dve.wait_ge(m_step, b.count(4, 2))
                        nc.vector.tensor_copy(mparts[b.two][:, 1, :], mrest[b.two][:, :]).then_inc(m_step, 1)
                    b = st.batch(slot, J_O)
                    if b:
                        dve.wait_ge(o_ps, b.count(1, 1))
                        nc.vector.reciprocal(rden[b.two][:, :, :],
                                             misc[slot % 2][:, :].rearrange("p (h c) -> p h c", c=16)[:, :, DK:DK + 1]
                                              ).then_inc(rden_ready, 1)
                    b = st.batch(slot, T_LN3_STATS)
                    if b:
                        dve.wait_ge(x1_ready, b.count(1, 1))
                        stats_of(2, b, x1[b.four])
                    for k in range(0, LEVELS, 2):
                        b = st.batch(slot, T_TREE + k // 2)
                        if b:
                            tree_level(b, k)
                    for n in range(UNITS):
                        b = st.batch(slot, T_MAX + n)
                        if b:
                            g, kind = n // 3, n % 3
                            if b.has(2):
                                dve.wait_ge(m_ps, b.count(1, -1))
                            dve.wait_ge(smax_ps, b.count(UNITS, n + 1))
                            if kind == 0 and g in MASKED_BY_PE:
                                nc.vector.tensor_reduce(mx[b.two][:, 4 * g:4 * g + 4, 0],
                                                        smax[n % 3][:, :].rearrange("p (h t) -> p h t", h=4),
                                                        AX_X, ALU.max).then_inc(max_done, 1)
                            else:
                                if n >= 4 or b.has(1):
                                    dve.wait_ge(max_done, b.count(UNITS, n - 2))
                                dve.nop(nofuse=True)
                                if kind == 0:
                                    for j in range(4):
                                        last = nc.vector.tensor_tensor_reduce(
                                            masked1[:, j, :], smax[n % 3][:, 128 * j:128 * j + 128], mask2[:, 1, :], 1.0,
                                            MASKED, ALU.add, ALU.max, mx[b.two][:, 4 * g + j, 0:1])
                                for ab in range(2 if kind else 0):
                                    h = 4 * g + 2 * (kind - 1) + ab
                                    last = nc.vector.tensor_tensor_reduce(
                                        masked2[:, kind - 1, ab, :], smax[n % 3][:, 256 * ab:256 * ab + 256],
                                        mask2[:, :, :].rearrange("p t n -> p (t n)"), 1.0,
                                        MASKED, ALU.add, ALU.max, mx[b.two][:, h, 1:2])
                                last.then_inc(max_done, 1)
                    b = st.batch(slot, T_LN1_STATS)
                    if b:
                        aggregate(0, b)
                    b = st.batch(slot, J_M)
                    if b:
                        dve.wait_ge(m_step, b.count(4, 1))
                        nc.vector.tensor_tensor(mrest[b.two][:, :], misc[J_M % 2][0:32, 0:128], mparts[b.two][:, 0, :],
                                                ALU.subtract).then_inc(m_step, 1)
                    b = st.batch(slot, J_O)
                    if b:
                        dve.wait_ge(rden_ready, b.count(1, 1))
                        if b.has(2):
                            dve.wait_ge(oT_ps, b.count(1, -1))
                        nc.vector.tensor_tensor(onorm[b.two][:, :, :, :].rearrange("p t h d -> p (t h) d"),
                                                misc[slot % 2][:, :].rearrange("p (h c) -> p h c", c=16)[:, :, 0:DK],
                                                rden[b.two][:, :, :].broadcast_to([128, 2 * HEADS, DK]),
                                                ALU.mult).then_inc(onorm_ready, 1)
                    b = st.batch(slot, T_LN3_STATS)
                    if b:
                        aggregate(2, b)
                    for k in range(1, LEVELS, 2):
                        b = st.batch(slot, T_TREE + k // 2)
                        if b:
                            tree_level(b, k)
                    b = st.batch(slot, T_STACK)
                    if b:
                        dve.wait_ge(lo_ready, b.count(1, 1))
                        for ab in range(2):
                            rows = slice(64 * ab, 64 * ab + 64)
                            nc.vector.tensor_copy(qsec[b.two][rows, ab, :, :].rearrange("p j t -> p (j t)"),
                                                  parts[b.two][rows, 0:3, :].rearrange("p j t -> p (j t)")
                                                  ).then_inc(qsec_ready, 1)

        @block.tensor
        def _(pe):
            def mm(dst, lhsT, rhs, start, stop):
                return nc.tensor.matmul(dst, lhsT, rhs, start=start, stop=stop, skip_group_check=True)

            pe.wait_ge(const_ready, 7)
            pe.wait_ge(w_loaded, 160)
            for j in range(4):
                last = nc.tensor.transpose(misc[0][:, 128 * j:128 * j + 128], wraw[:, j, :], ident[:, :])
            last.then_inc(w_turned, 1)
            for j, w in enumerate((W_R0, W_L0, W_L1, W_OUT)):
                last = nc.tensor.transpose(misc[1][:, 128 * j:128 * j + 128], wraw[:, w, :], ident[:, :])
            last.then_inc(w_turned, 1)
            nc.tensor.transpose(smax[0][:, 0:127], rraw[:, :], ident[0:127, 0:127]).then_inc(w_turned, 1)
            pe.wait_ge(w_copied, 8)
            pe.wait_ge(centre_step, 3)
            mm(smax[1][:, 0:NODES], wqc[:, :], rT[:, 0:NODES], True, True).then_inc(w_fused, 1)
            leaves = wT[:, W_L0:W_L1 + 1, :].rearrange("p a n -> p (a n)")
            pe.wait_ge(bias_loaded, 16)
            for side in range(2):
                dst = sexp[0][:, 128 * side:128 * side + 128]
                mm(dst, leaves[:, side::2], wT[:, W_OUT, :], True, False)
                last = mm(dst, ones1[:, :], bias0[:, :], False, True)
            last.then_inc(w_fused, 1)

            def causal_mask(dst, heads):
                mm(dst, identb[:, :], mask[:, :].unsqueeze(1).broadcast_to([128, heads, 128]), True, False)

            misc_read = {J_XT: (xT_ready, 1, 1), J_QK: (rest_ready, 1, 1), J_V: (v_ready, 1, 1), J_M: (m_step, 4, 2),
                         J_O: (onorm_ready, 1, 1), J_OT: (oT_ready, 1, 1),
                         J_Y: (y_ready, 1, 1), J_X1T: (x1T_ready, 1, 1), J_Z: (u_ready, 1, 1),
                         J_LPT: (lpT_ready, 1, 1), J_RET: (ret_ready, 1, 1)}

            for st in steps(pe):
                for slot in range(SLOTS):
                    bank = misc[slot % 2]
                    if any(st.batch(slot, t) for t in MISC_JOBS):
                        for before in range(slot - 2, slot - SLOTS - 1, -2):
                            t = next((t for t in MISC_JOBS if (t - before) % SLOTS == 0), None)
                            b = t and st.batch(before, t)
                            if b:
                                read, per, plus = misc_read[t]
                                pe.wait_ge(read, b.count(per, plus))
                                break

                    b = st.batch(slot, J_XT)
                    if b:
                        pe.wait_ge(xn_ready, b.count(2, 2))
                        for t in range(2):
                            last = nc.tensor.transpose(bank[:, 128 * t:128 * t + 128], xn[b.two][:, t, :], ident[:, :])
                        last.then_inc(xT_ps, 1)
                    b = st.batch(slot, J_QK)
                    if b:
                        pe.wait_ge(xT_ready, b.count(1, 1))
                        for j in range(2):
                            last = mm(bank[:, 256 * j:256 * j + 256], wqk[:, j, :], xT[b.two][:, :], True, True)
                        last.then_inc(qk_ps, 1)
                    b = st.batch(slot, J_V)
                    if b:
                        pe.wait_ge(xT_ready, b.count(1, 1))
                        for t in range(2):
                            last = mm(bank[:, 128 * t:128 * t + 128], xT[b.two][:, 128 * t:128 * t + 128],
                                      wT[:, W_V, :], True, True)
                        last.then_inc(v_ps, 1)
                    b = st.batch(slot, J_M)
                    if b:
                        pe.wait_ge(max_done, b.count(UNITS, UNITS))
                        nc.tensor.transpose(bank[0:32, 0:128], mx[b.two][:, :, :].rearrange("p h t -> p (h t)"),
                                            ident[:, :]).then_inc(m_ps, 1)
                    b = st.batch(slot, J_O)
                    if b:
                        pe.wait_ge(oraw_ready, b.count(1, 1))
                        for t in range(2):
                            for half in range(2):
                                last = nc.tensor.transpose(bank[:, 256 * t + 128 * half:256 * t + 128 * half + 128],
                                                           oraw[b.two][:, 256 * half + 128 * t:256 * half + 128 * t + 128],
                                                           ident[:, :])
                        last.then_inc(o_ps, 1)
                    b = st.batch(slot, J_OT)
                    if b:
                        pe.wait_ge(onorm_ready, b.count(1, 1))
                        for t in range(2):
                            last = nc.tensor.transpose(bank[:, 128 * t:128 * t + 128],
                                                       onorm[b.two][:, t, :, :].rearrange("p h d -> p (h d)"), ident[:, :])
                        last.then_inc(oT_ps, 1)
                    b = st.batch(slot, J_Y)
                    if b:
                        pe.wait_ge(oT_ready, b.count(1, 1))
                        if not b.has(1):
                            pe.wait_ge(w_ready, 2)
                        for t in range(2):
                            last = mm(bank[:, 128 * t:128 * t + 128], oT[b.two][:, 128 * t:128 * t + 128],
                                      woc[:, :], True, True)
                        last.then_inc(y_ps, 1)
                    b = st.batch(slot, J_X1T)
                    if b:
                        pe.wait_ge(x1_ready, b.count(1, 1))
                        for t in range(2):
                            last = nc.tensor.transpose(bank[:, 128 * t:128 * t + 128], x1[b.four][:, t, :], ident[:, :])
                        last.then_inc(x1T_ps, 1)
                    b = st.batch(slot, J_Z)
                    if b:
                        pe.wait_ge(x1T_ready, b.count(1, 1))
                        for t in range(2):
                            last = mm(bank[:, GATES * t:GATES * t + GATES], x1T[b.two][:, 128 * t:128 * t + 128],
                                      wg[:, :], True, True)
                        last.then_inc(z_ps, 1)
                    b = st.batch(slot, J_LPT)
                    if b:
                        pe.wait_ge(tree_step, b.count(TREE, TREE))
                        for t in range(2):
                            nc.tensor.transpose(bank[:, 256 * t:256 * t + 128], tree[b.two][:, t, HALF:2 * HALF], ident[:, :])
                            last = nc.tensor.transpose(bank[:, 256 * t + 128:256 * t + 256], right[b.two][:, t, :], ident[:, :])
                        last.then_inc(lpT_ps, 1)
                    b = st.batch(slot, J_RET)
                    if b:
                        pe.wait_ge(lpT_ready, b.count(1, 1))
                        for t in range(2):
                            mm(bank[:, 128 * t:128 * t + 128], lpT[b.two][:, t, 0, :], lva[:, :], True, False)
                            last = mm(bank[:, 128 * t:128 * t + 128], lpT[b.two][:, t, 1, :], lvb[:, :], False, True)
                        last.then_inc(ret_ps, 1)

                    for n in range(UNITS):
                        b = st.batch(slot, T_MAX + n)
                        if b:
                            g, kind = n // 3, n % 3
                            if n == 0:
                                pe.wait_ge(stacked[b.four], b.turns_of(4, 16 * 12))
                            if n >= 3 or b.has(1):
                                pe.wait_ge(max_done, b.count(UNITS, n - 2))
                            S, Q, K = smax[n % 3], qs[b.four], kd[b.four]
                            if kind == 0:
                                if g in MASKED_BY_PE:
                                    causal_mask(S[:, :], 4)
                                for j in range(4):
                                    hp, ab = 2 * g + j // 2, j % 2
                                    last = mm(S[:, 128 * j:128 * j + 128], Q[0:STACK, hp, ab, 0:128],
                                              K[0:STACK, hp, 0:128], g not in MASKED_BY_PE, True)
                            else:
                                hp = 2 * g + kind - 1
                                for ab in range(2):
                                    last = mm(S[:, 256 * ab:256 * ab + 256], Q[0:STACK, hp, ab, 128:256],
                                              K[0:STACK, hp, :], True, True)
                            last.then_inc(smax_ps, 1)
                    for n in range(UNITS):
                        b = st.batch(slot, T_EXP + n)
                        if b:
                            g, kind = n // 3, n % 3
                            if n == 0:
                                pe.wait_ge(mrows_in[b.two], b.turns_of(2, 48))
                                if not b.has(4):
                                    pe.wait_ge(kd_set, 4)
                            if n >= 2 or b.has(1):
                                pe.wait_ge(exp_done, b.count(UNITS, n - 1))
                            S, Q, K = sexp[n % 2], qs[b.four], kd[b.four]
                            if kind < 2:
                                hp = 2 * g + kind
                                last = mm(S[:, :], K[0:STACK + MROWS, hp, 0:128],
                                          Q[0:STACK + MROWS, hp, :, :].rearrange("p s t -> p (s t)"), True, True)
                            else:
                                for j in range(2):
                                    hp = 2 * g + j
                                    last = mm(S[:, 256 * j:256 * j + 256], K[0:STACK + MROWS, hp, 128:256],
                                              Q[0:STACK + MROWS, hp, :, 128:256], True, True)
                            last.then_inc(sexp_ps, 1)
                    for j in range(4):
                        b = st.batch(slot, T_PV[j])
                        if b:
                            half, ab = j // 2, j % 2
                            if ab == 0:
                                pe.wait_ge(causal_done, b.count(8, 4 * half + 4))
                            if j == 0:
                                pe.wait_ge(v_ready, b.count(1, 1))
                                if b.has(1):
                                    pe.wait_ge(oraw_ready, b.count(1, 0))
                            P, V, O, c = probs[b.two], vaug[b.four], pvps, 256 * half
                            for q in range(4):
                                hp = 4 * half + q
                                mm(O[32 * q:32 * q + 32, c:c + 256], V[:, 0, hp, ab, :],
                                   P[:, 3 * (hp // 2) + hp % 2, 256 * ab:256 * ab + 256], ab == 0, False)
                            for q in range(4):
                                hp = 4 * half + q
                                block = 128 * (2 * (hp % 2) + ab)
                                last = mm(O[32 * q:32 * q + 32, c + 128:c + 256], V[:, 1, hp, ab, :],
                                          P[:, 3 * (hp // 2) + 2, block:block + 128], False, ab == 1)
                            last.then_inc(pv_ps, 1)


_INS = ['L0_attn_x', 'L0_attn_w_qkv', 'L0_attn_w_o', 'L0_ffn_Wq', 'L0_ffn_routers', 'L0_ffn_leaf_keys',
        'L0_ffn_leaf_values', 'L0_ffn_Wout_w', 'L0_ffn_Wout_b']
_OUTS = [((BATCHES, SEQ, D), 'float32')]


def kernel(**inputs):
    import numpy as _np
    import concourse.bacc as _bacc
    from concourse import mybir as _mybir
    from concourse.bass_utils import run_bass_kernel_spmd as _run

    nc = _bacc.Bacc("TRN2", target_bir_lowering=False, num_devices=1)
    arrays, args = {}, []
    for name in _INS:
        a = _np.ascontiguousarray(inputs[name])
        arrays[f"in_{name}_dram"] = a
        args.append(nc.dram_tensor(f"in_{name}_dram", a.shape, _mybir.dt.from_np(a.dtype), kind="ExternalInput").ap())
    for i, (shape, dtype) in enumerate(_OUTS):
        dt = _mybir.dt.from_np(_np.dtype(dtype))
        args.append(nc.dram_tensor(f"out_{i}_dram", shape, dt, kind="ExternalOutput").ap())
    sandwich_kernel(nc, *args)
    r = _run(nc, [arrays], core_ids=[0])
    got = tuple(r.results[0][f"out_{i}_dram"] for i in range(len(_OUTS)))
    return got[0]
```
